# Optimizing a Trainium2 kernel written in Bass

```python
import numpy as np
import jax
import jax.numpy as jnp

def _softmax(x, axis=-1):
    return jax.nn.softmax(x, axis=axis)

def _gelu(x):
    return jax.nn.gelu(x, approximate=True)

def _silu(x):
    return jax.nn.silu(x)

def _sigmoid(x):
    return jax.nn.sigmoid(x)

def _layernorm(x, axis=-1, eps=1e-05):
    m = jnp.mean(x, axis=axis, keepdims=True)
    v = jnp.var(x, axis=axis, keepdims=True)
    return (x - m) / jnp.sqrt(v + eps)

def _scatter_add(tgt, idx, src, axis=0):
    return tgt.at[idx].add(src)

def _segment_sum(src, seg, n):
    return jax.ops.segment_sum(src, seg, n)
kernel_name = 'mk_seq_preln_d1_jaxref_r8_f909ba'

def setup_inputs(seed: int=0):
    np.random.seed(seed)
    _w = jnp.asarray

    def _L0_attn_setup():
        import jax, jax.numpy as jnp
        import numpy as np
        D_MODEL = 128
        N_HEADS = 16
        D_K = D_MODEL // N_HEADS
        B, S = (4, 256)
        key = jax.random.key(seed)
        ks = jax.random.split(key, 9)
        sc = 1.0 / np.sqrt(D_MODEL)
        return {'x': jax.random.normal(ks[0], (B, S, D_MODEL), dtype=jnp.float32), 'Wq': jax.random.normal(ks[1], (D_MODEL, D_MODEL), dtype=jnp.float32) * sc, 'bq': jax.random.normal(ks[2], (D_MODEL,), dtype=jnp.float32) * 0.02, 'Wk': jax.random.normal(ks[3], (D_MODEL, D_MODEL), dtype=jnp.float32) * sc, 'bk': jax.random.normal(ks[4], (D_MODEL,), dtype=jnp.float32) * 0.02, 'Wv': jax.random.normal(ks[5], (D_MODEL, D_MODEL), dtype=jnp.float32) * sc, 'bv': jax.random.normal(ks[6], (D_MODEL,), dtype=jnp.float32) * 0.02, 'Wo': jax.random.normal(ks[7], (D_MODEL, D_MODEL), dtype=jnp.float32) * sc, 'bo': jax.random.normal(ks[8], (D_MODEL,), dtype=jnp.float32) * 0.02}
    _L0_attn_in = _L0_attn_setup()

    def _L0_ffn_setup():
        import jax, jax.numpy as jnp
        import numpy as np
        B, S, D, F, E = (8, 128, 128, 512, 8)
        EPS = 1e-05
        key = jax.random.key(seed)
        ks = jax.random.split(key, 4)
        s = 0.02
        return {'input_features': jax.random.normal(ks[0], (B, S, D), jnp.float32), 'centroids': jax.random.normal(ks[1], (E, D), jnp.float32) * 0.1, 'ln_g': jnp.ones((E, D), jnp.float32), 'ln_b': jnp.zeros((E, D), jnp.float32), 'w1': jax.random.normal(ks[2], (E, D, F), jnp.float32) * s, 'b1': jnp.zeros((E, F), jnp.float32), 'w2': jax.random.normal(ks[3], (E, F, D), jnp.float32) * s, 'b2': jnp.zeros((E, D), jnp.float32)}
    _L0_ffn_in = _L0_ffn_setup()
    _d = {'L0_attn_x': _L0_attn_in['x'], 'L0_attn_Wq': _L0_attn_in['Wq'], 'L0_attn_bq': _L0_attn_in['bq'], 'L0_attn_Wk': _L0_attn_in['Wk'], 'L0_attn_bk': _L0_attn_in['bk'], 'L0_attn_Wv': _L0_attn_in['Wv'], 'L0_attn_bv': _L0_attn_in['bv'], 'L0_attn_Wo': _L0_attn_in['Wo'], 'L0_attn_bo': _L0_attn_in['bo'], 'L0_ffn_centroids': _L0_ffn_in['centroids'], 'L0_ffn_ln_g': _L0_ffn_in['ln_g'], 'L0_ffn_ln_b': _L0_ffn_in['ln_b'], 'L0_ffn_w1': _L0_ffn_in['w1'], 'L0_ffn_b1': _L0_ffn_in['b1'], 'L0_ffn_w2': _L0_ffn_in['w2'], 'L0_ffn_b2': _L0_ffn_in['b2']}
    _x0 = _d['L0_attn_x']
    _d['L0_attn_x'] = jax.random.normal(jax.random.fold_in(jax.random.key(seed), 1), (4, 1024, 128), dtype=_x0.dtype)
    del _x0
    return _d

def reference(L0_attn_x, L0_attn_Wq, L0_attn_bq, L0_attn_Wk, L0_attn_bk, L0_attn_Wv, L0_attn_bv, L0_attn_Wo, L0_attn_bo, L0_ffn_centroids, L0_ffn_ln_g, L0_ffn_ln_b, L0_ffn_w1, L0_ffn_b1, L0_ffn_w2, L0_ffn_b2):

    def _L0_attn_ref(x, Wq, bq, Wk, bk, Wv, bv, Wo, bo):
        import jax, jax.numpy as jnp
        import numpy as np
        D_MODEL = 128
        N_HEADS = 16
        D_K = D_MODEL // N_HEADS
        B, S = (4, 256)
        b, s, _ = x.shape
        q = (x @ Wq + bq).reshape(b, s, N_HEADS, D_K).transpose(0, 2, 1, 3)
        k = (x @ Wk + bk).reshape(b, s, N_HEADS, D_K).transpose(0, 2, 1, 3)
        v = (x @ Wv + bv).reshape(b, s, N_HEADS, D_K).transpose(0, 2, 1, 3)
        scores = jnp.einsum('bhqd,bhkd->bhqk', q, k) / jnp.sqrt(jnp.float32(D_K))
        attn = jax.nn.softmax(scores, axis=-1)
        out = jnp.einsum('bhqk,bhkd->bhqd', attn, v)
        out = out.transpose(0, 2, 1, 3).reshape(b, s, D_MODEL)
        return out @ Wo + bo

    def _L0_ffn_ref(input_features, centroids, ln_g, ln_b, w1, b1, w2, b2):
        import jax, jax.numpy as jnp
        import numpy as np
        B, S, D, F, E = (8, 128, 128, 512, 8)
        EPS = 1e-05
        x = input_features.reshape(-1, D)
        aff = jax.lax.stop_gradient(x @ centroids.T)
        eid = jnp.argmax(aff, axis=-1)
        alpha = jax.nn.sigmoid(jnp.sum(x * centroids[eid], axis=-1, keepdims=True))
        mu = jnp.mean(x, axis=-1, keepdims=True)
        var = jnp.mean((x - mu) ** 2, axis=-1, keepdims=True)
        xn = (x - mu) * jax.lax.rsqrt(var + EPS)
        xln = xn * ln_g[eid] + ln_b[eid]
        onehot = jax.nn.one_hot(eid, E, dtype=x.dtype)
        ffn = jnp.zeros_like(x)
        for e in range(E):
            h = jax.nn.relu(xln @ w1[e] + b1[e])
            ffn = ffn + onehot[:, e:e + 1] * (h @ w2[e] + b2[e])
        out = x + alpha * ffn
        return out.reshape(input_features.shape)
    x = L0_attn_x
    x = x + _L0_attn_ref(_layernorm(x, axis=-1), L0_attn_Wq, L0_attn_bq, L0_attn_Wk, L0_attn_bk, L0_attn_Wv, L0_attn_bv, L0_attn_Wo, L0_attn_bo)
    x = x + _L0_ffn_ref(_layernorm(x, axis=-1), L0_ffn_centroids, L0_ffn_ln_g, L0_ffn_ln_b, L0_ffn_w1, L0_ffn_b1, L0_ffn_w2, L0_ffn_b2)
    return x

_drawn_inputs = setup_inputs


def setup_inputs(seed=0):
    import zlib

    import numpy as np

    out = dict(_drawn_inputs(seed))
    spreads = {'L0_ffn_ln_g': (1.0, 0.6),
     'L0_ffn_ln_b': (0.0, 2.0),
     'L0_ffn_b1': (0.0, 0.638),
     'L0_ffn_b2': (0.0, 0.1)}
    factors = {'L0_attn_bq': 21.886, 'L0_attn_bk': 64.0}
    for name, (base, spread) in spreads.items():
        noise = np.random.default_rng([zlib.crc32(name.encode()), seed]).standard_normal(out[name].shape)
        drawn = base * np.exp(spread * noise) if base else spread * noise
        out[name] = jnp.asarray(drawn.astype(out[name].dtype))
    for name, factor in factors.items():
        out[name] = (out[name] * factor).astype(out[name].dtype)
    return out
```

```python
import concourse.bass as bass
import concourse.mybir as mybir
from contextlib import ExitStack

F32 = mybir.dt.float32
BF16 = mybir.dt.bfloat16
I32 = mybir.dt.int32
ALU = mybir.AluOpType
ACT = mybir.ActivationFunctionType
AX = mybir.AxisListType

P = 128
B, S, D = 4, 1024, 128
H = 16
DK = D // H
E, F = 8, 512
EPS = 1e-5
TPB = S // P
T = B * TPB
NU = B * H
NPAIR = NU // 2
PARTS = 3
ROWS = PARTS * PARTS * DK
SROWS = ROWS + PARTS
SLOTS = 4
QUADS = NU // SLOTS
VC = 32
QUART = S // 4
HALF = 512
FC = F // P
SORTED = T + E - 1
SCALE = float(DK) ** -0.5


def ge(eng, sem, value):
    if isinstance(value, int) and value <= 0:
        return
    eng.wait_ge(sem, value)


def bare(eng, held, *waits):
    waits = [(s, v) for s, v in waits if not (isinstance(v, int) and v <= 0)]
    waits = [(s, v if isinstance(v, int) else eng.to_reg(v)) for s, v in waits]
    eng.wait_ge(*held)
    for s, v in waits:
        eng.wait_ge(s, v)


def chain(eng, sem, base=0):
    n = [0]

    def step(ins):
        n[0] += 1
        ins.then_inc(sem, 1)
        eng.wait_ge(sem, base + n[0])
    step.count = n
    return step


def build(nc, x, Wq, bq, Wk, bk, Wv, bv, Wo, bo, cent, ln_g, ln_b, w1, b1, w2, b2, out):
    ctx = ExitStack()
    with ctx:
        def sb(name, shape, dt=F32):
            return ctx.enter_context(nc.sbuf_tensor(name, shape, dt))

        def sem(name):
            return ctx.enter_context(nc.semaphore(name))

        q_rows = nc.dram_tensor("q_rows", (B, P, PARTS * PARTS * S), BF16, kind="Internal").ap()
        k_rows = nc.dram_tensor("k_rows", (B, P, PARTS * PARTS * S), BF16, kind="Internal").ap()
        q_unit = q_rows.rearrange("b (h d) (r s) -> (b h) (d r) s", d=DK, s=S)
        k_unit = k_rows.rearrange("b (h d) (r s) -> (b h) (d r) s", d=DK, s=S)
        sorted_x = nc.dram_tensor("sorted_x", (SORTED * P, D), F32, kind="Internal").ap()
        sorted_y = nc.dram_tensor("sorted_y", (SORTED * P, D), F32, kind="Internal").ap()

        wq_s, wk_s, wv_s, wo_s = (sb(n, [P, D]) for n in ("wq_s", "wk_s", "wv_s", "wo_s"))
        bq_s, bk_s = sb("bq_s", [P, 1]), sb("bk_s", [P, 1])
        bv_s, bo_s = sb("bv_s", [1, D]), sb("bo_s", [1, D])
        cent_s, centT = sb("cent_s", [E, D]), sb("centT", [P, E])
        gb_s, gbT = sb("gb_s", [2 * E, D]), sb("gbT", [P, 2 * E])
        b1_s, b1T = sb("b1_s", [E * FC, P]), sb("b1T", [P, E * FC])
        b2_s = sb("b2_s", [1, E * D])
        w1_s, w2_s = sb("w1_s", [P, E * F]), sb("w2_s", [P, E * F])
        ident, identb = sb("ident", [P, P]), sb("identb", [P, P], BF16)
        ones_row = sb("ones_row", [1, P])
        before = sb("before", [P, P], BF16)
        onesb = sb("onesb", [P, P], BF16)
        zeros = sb("zeros", [P, D])

        X = sb("X", [P, T, D])
        Vall = sb("Vall", [P, NU * TPB * DK])
        A = sb("A", [P, T, D])
        U2 = sb("U2", [P, T, D])
        XN = sb("XN", [P, T, D])
        stats, mv = sb("stats", [P, TPB, 6]), sb("mv", [P, TPB, 2])
        rstd, vpe, root, newt = (sb(n, [P, TPB]) for n in ("rstd", "vpe", "root", "newt"))
        xnT = sb("xnT", [P, S])
        full = sb("full", [P, 2, S])
        rest = sb("rest", [P, 2, S])
        parts = sb("parts", [P, 2, PARTS, S], BF16)
        QA, KA = sb("QA", [P, SLOTS, S], BF16), sb("KA", [P, SLOTS, S], BF16)
        Vst = sb("Vst", [P, SLOTS, TPB, VC])
        probs = sb("probs", [P, 2, S])
        max2 = sb("max2", [P, 2, TPB, 2])
        negmax, mrest = sb("negmax", [P, TPB]), sb("mrest", [P, 2, TPB])
        mparts = sb("mparts", [P, PARTS, TPB], BF16)
        shiftT = sb("shiftT", [PARTS * TPB, SLOTS, P], BF16)
        O_s = sb("O_s", [P, QUART])
        rec = sb("rec", [P, TPB, 2])

        aff, eq = sb("aff", [P, T, E]), sb("eq", [P, T, E])
        top, alpha, pick = sb("top", [P, T]), sb("alpha", [P, T]), sb("pick", [P, T])
        first_w = sb("first_w", [P, E])
        hot, hotb = sb("hot", [P, T, E]), sb("hotb", [P, T, E], BF16)
        tot, cum = sb("tot", [P, E, T]), sb("cum", [P, E, T])
        zrow = sb("zrow", [P, E * T])
        cnt, cnti = sb("cnt", [P, E]), sb("cnti", [P, E], I32)
        padded, ends, start = sb("padded", [P, E]), sb("ends", [P, E]), sb("start", [P, E])
        cstart = sb("cstart", [P, E])
        place, slot_f, slot_i = sb("place", [P, T, E]), sb("slot_f", [P, T]), sb("slot_i", [P, T], I32)
        tile_at, tile_cmp = sb("tile_at", [P, SORTED]), sb("tile_cmp", [P, SORTED, E])
        tile_ef, tile_e = sb("tile_ef", [P, SORTED]), sb("tile_e", [P, SORTED], I32)

        xs = sb("xs", [P, 2, D])
        xsT = sb("xsT", [P, 2, P])
        w1r, w2r = full[:, :, 0:F], full[:, :, F:2 * F]
        gbr, b1r, b2r = sb("gbr", [P, 2, 2]), sb("b1r", [P, 2, FC]), sb("b2r", [1, 2, D])
        hT = rest[:, :, 0:F]
        ys = sb("ys", [P, 2, D])
        yg = U2

        ST = [ctx.enter_context(nc.psum_tensor(f"ST{i}", [P, S], F32)) for i in range(2)]
        SC = [ctx.enter_context(nc.psum_tensor(f"SC{i}", [P, HALF], F32)) for i in range(2)]
        OB = ctx.enter_context(nc.psum_tensor("OB", [P, HALF], F32))
        MB = ctx.enter_context(nc.psum_tensor("MB", [P, HALF], F32))
        MT = MB[0:PARTS * TPB, 2 * P:2 * P + P // 2].bitcast(BF16)

        x_in, w_in, ffn_in = sem("x_in"), sem("w_in"), sem("ffn_in")
        consts, table_in, table_T, table_out = sem("consts"), sem("table_in"), sem("table_T"), sem("table_out")
        pool_step, dve_step, act_step = sem("pool_step"), sem("dve_step"), sem("act_step")
        var_ok, root_ok = sem("var_ok"), sem("root_ok")
        normed, xnT_ps, xnT_sb = sem("normed"), sem("xnT_ps"), sem("xnT_sb")
        qk_ps, v_ps, full_ok, v_ok = sem("qk_ps"), sem("v_ps"), sem("full_ok"), sem("v_ok")
        part1, rest1, part2, part3, rows_out = (sem(n) for n in ("part1", "rest1", "part2", "part3", "rows_out"))
        qk_loaded = [sem(f"qk_loaded{j}") for j in range(SLOTS)]
        shift_loaded = [sem(f"shift_loaded{j}") for j in range(SLOTS)]
        s_written, s_read = sem("s_written"), sem("s_read")
        st_written, p_ready, pv_done = sem("st_written"), sem("p_ready"), sem("pv_done")
        v_ready, max_ready, mparts_ready = sem("v_ready"), sem("max_ready"), sem("mparts_ready")
        mT_written, mT_copied = sem("mT_written"), sem("mT_copied")
        o_copied, o_transposed, o_rec, o_normed = (sem(n) for n in ("o_copied", "o_transposed", "o_rec", "o_normed"))
        a_ps, a_sb, y_ps, x1_ok = sem("a_ps"), sem("a_sb"), sem("y_ps"), sem("x1_ok")
        u_ok, u_ps, u_sb, aff_ps, aff_ok, xn_ok = (sem(n) for n in ("u_ok", "u_ps", "u_sb", "aff_ps", "aff_ok", "xn_ok"))
        res_ok, gate_ok, hot_ok, rank_ps, slots_ok = (sem(n) for n in ("res_ok", "gate_ok", "hot_ok", "rank_ps", "slots_ok"))
        zeroed, scattered = sem("zeroed"), sem("scattered")
        xs_in = [sem(f"xs_in{i}") for i in range(2)]
        ys_out = [sem(f"ys_out{i}") for i in range(2)]
        xs_ps, xs_sb, ring_ok, h_ps, h_act, h_dve, f_ps, f_sb = (
            sem(n) for n in ("xs_ps", "xs_sb", "ring_ok", "h_ps", "h_act", "h_dve", "f_ps", "f_sb"))
        gathered, final_ok, out_done = sem("gathered"), sem("final_ok"), sem("out_done")

        W_LOADS, FFN_LOADS, CONSTS = 8, 7, 11
        TABLES = 3
        block = ctx.enter_context(nc.Block())

        @block.sync
        def _(sp):
            sp.dma_start(X[:], x.rearrange("b (t p) d -> p (b t) d", p=P)).then_inc(x_in, 16)
            for dst, src in ((wq_s, Wq), (wk_s, Wk), (wv_s, Wv), (wo_s, Wo)):
                sp.dma_start(dst[:], src).then_inc(w_in, 16)
            for dst, src in ((bq_s, bq), (bk_s, bk)):
                sp.dma_start(dst[:], src.rearrange("(p a) -> p a", a=1)).then_inc(w_in, 16)
            for dst, src in ((bv_s, bv), (bo_s, bo)):
                sp.dma_start(dst[:], src.rearrange("(a n) -> a n", a=1)).then_inc(w_in, 16)
            sp.dma_start(cent_s[:], cent).then_inc(ffn_in, 16)
            sp.dma_start(gb_s[0:E, :], ln_g).then_inc(ffn_in, 16)
            sp.dma_start(gb_s[E:2 * E, :], ln_b).then_inc(ffn_in, 16)
            sp.dma_start(b1_s[:], b1.rearrange("e (c p) -> (e c) p", p=P)).then_inc(ffn_in, 16)
            sp.dma_start(b2_s[:], b2.rearrange("e d -> (e d)").rearrange("(a n) -> a n", a=1)).then_inc(ffn_in, 16)
            sp.dma_start(w1_s[:].rearrange("p (e f) -> p e f", e=E), w1.rearrange("e p f -> p e f")).then_inc(ffn_in, 16)
            sp.dma_start(w2_s[:].rearrange("p (e c d) -> p e c d", e=E, c=FC),
                         w2.rearrange("e (c p) d -> p e c d", p=P)).then_inc(ffn_in, 16)

            with sp.Fori(0, B) as b:
                sp.wait_ge(part3, 2 * b + 2)
                for i in range(PARTS):
                    sp.dma_start(q_rows[bass.ds(b, 1), :, i * PARTS * S:(i + 1) * PARTS * S]
                                 .rearrange("a p (j s) -> (a p) j s", j=PARTS),
                                 parts[:, 0, i].unsqueeze(1).to_broadcast([P, PARTS, S])).then_inc(rows_out, 16)
                sp.dma_start(k_rows[bass.ds(b, 1)].rearrange("a p (i n) -> (a p) i n", i=PARTS),
                             parts[:, 1].rearrange("p j s -> p (j s)").unsqueeze(1).to_broadcast([P, PARTS, PARTS * S])
                             ).then_inc(rows_out, 16)
            sp.wait_ge(rows_out, 16 * (PARTS + 1) * B)
            sp.wait_ge(consts, CONSTS)

            def load(n, j):
                ge(sp, st_written, TPB * (n - SLOTS + 1))
                sp.dma_start(QA[0:ROWS, j], q_unit[bass.ds(n, 1)].rearrange("a r s -> (a r) s")).then_inc(qk_loaded[j], 16)
                sp.dma_start(KA[0:ROWS, j], k_unit[bass.ds(n, 1)].rearrange("a r s -> (a r) s")).then_inc(qk_loaded[j], 16)

            def shift(n, j):
                sp.wait_ge(mT_copied, n + 1)
                for i in range(PARTS):
                    sp.dma_start(QA[ROWS + i:ROWS + i + 1, j, :].rearrange("a (t q) -> a t q", t=TPB),
                                 shiftT[TPB * i:TPB * (i + 1), j, :]).then_inc(shift_loaded[j], 16)

            for n in range(SLOTS):
                load(n, n)
            shift(0, 0)

            def slot(u, j, last=False):
                if not (last and j > 0) and not (isinstance(u, int) and u == 0):
                    load(u + 3, (j + 3) % SLOTS)
                if not (last and j == SLOTS - 1):
                    shift(u + 1, (j + 1) % SLOTS)

            for j in range(SLOTS):
                slot(j, j)
            with sp.Fori(1, QUADS - 1) as q:
                for j in range(SLOTS):
                    slot(q * SLOTS + j, j)
            for j in range(SLOTS):
                slot(NU - SLOTS + j, j, last=True)

            sp.wait_ge(scattered, 16 * T)

            def load_x(n, i):
                ge(sp, xs_ps, n - 1)
                sp.dma_start(xs[:, i], sorted_x[bass.ds(n * P, P), :]).then_inc(xs_in[i], 16)

            def store_y(n, i):
                sp.wait_ge(f_sb, n + 1)
                sp.dma_start(sorted_y[bass.ds(n * P, P), :], ys[:, i]).then_inc(ys_out[i], 16)

            load_x(0, 0)
            load_x(1, 1)
            store_y(0, 0)
            load_x(2, 0)
            with sp.Fori(0, (SORTED - 3) // 2) as r:
                store_y(r * 2 + 1, 1)
                load_x(r * 2 + 3, 1)
                store_y(r * 2 + 2, 0)
                load_x(r * 2 + 4, 0)
            assert SORTED % 2 == 1
            store_y(SORTED - 2, 1)
            store_y(SORTED - 1, 0)

            for b in range(B):
                sp.wait_ge(final_ok, b + 1)
                sp.dma_start(out[b].rearrange("(t p) d -> p t d", p=P), yg[:, b * TPB:(b + 1) * TPB]).then_inc(out_done, 16)
            sp.wait_ge(out_done, 16 * B)
            for i in range(2):
                sp.wait_ge(ys_out[i], 16 * ((SORTED + 1 - i) // 2))
            sp.wait_ge(zeroed, 16 * SORTED)

        @block.gpsimd
        def _(pool):
            nc.gpsimd.memset(ident[:], 0.0).then_inc(pool_step, 1)
            nc.gpsimd.memset(identb[:], 0.0).then_inc(pool_step, 1)
            nc.gpsimd.memset(before[:], 1.0).then_inc(pool_step, 1)
            nc.gpsimd.memset(Vst[:], 0.0).then_inc(pool_step, 1)
            nc.gpsimd.memset(ones_row[:], 1.0).then_inc(consts, 1)
            nc.gpsimd.memset(onesb[:], 1.0).then_inc(consts, 1)
            nc.gpsimd.memset(zeros[:], 0.0).then_inc(consts, 1)
            nc.gpsimd.memset(zrow[:], 0.0).then_inc(consts, 1)
            nc.gpsimd.iota(first_w[:], [[-1, E]], base=E, channel_multiplier=0,
                           allow_small_or_imprecise_dtypes=True).then_inc(consts, 1)
            nc.gpsimd.iota(tile_at[:], [[P, SORTED]], base=0, channel_multiplier=0,
                           allow_small_or_imprecise_dtypes=True).then_inc(consts, 1)
            pool.wait_ge(pool_step, 4)
            for m in (ident, identb):
                nc.gpsimd.affine_select(out=m[:], in_=m[:], compare_op=ALU.not_equal, fill=1.0, base=0,
                                        pattern=[[-1, P]], channel_multiplier=1).then_inc(consts, 1)
            nc.gpsimd.affine_select(out=before[:], in_=before[:], compare_op=ALU.is_gt, fill=0.0, base=0,
                                    pattern=[[1, P]], channel_multiplier=-1).then_inc(consts, 1)
            for j in range(SLOTS):
                last = nc.gpsimd.memset(Vst[:, j, :, 2 * DK + j % 2:2 * DK + j % 2 + 1], 1.0)
                last.then_inc(consts if j == SLOTS - 1 else pool_step, 1)

            with pool.Fori(0, B) as b:
                for i in range(2):
                    pool.wait_ge(part1, 2 * b + 1 + i)
                    nc.gpsimd.tensor_tensor(rest[:, i], full[:, i], parts[:, i, 0], ALU.subtract).then_inc(rest1, 1)
                for i in range(2):
                    pool.wait_ge(part2, 2 * b + 1 + i)
                    nc.gpsimd.tensor_tensor(parts[:, i, 2], rest[:, i], parts[:, i, 1], ALU.subtract).then_inc(part3, 1)

            for n in range(SORTED):
                pool.dma_start(sorted_x[n * P:(n + 1) * P, :], zeros[:]).then_inc(zeroed, 16)

            pool.wait_ge(v_ok, 2 * B)

            MSTEPS = 3

            def unit(n, j):
                bare(pool, (v_ok, 2 * B), (pv_done, TPB * (n - SLOTS + 1)))
                nc.gpsimd.tensor_copy(Vst[:, j, :, (j % 2) * DK:(j % 2 + 1) * DK],
                                      Vall[:, bass.ds(n * (TPB * DK), TPB * DK)].rearrange("p (t d) -> p t d", d=DK)
                                      ).then_inc(v_ready, 1)
                bare(pool, (v_ok, 2 * B), (max_ready, n + 1), (mT_written, n))
                step = chain(pool, pool_step, POOL0 + n * MSTEPS)
                step(nc.gpsimd.tensor_copy(mparts[:, 0], negmax[:]))
                nc.gpsimd.tensor_tensor(mrest[:, 0], negmax[:], mparts[:, 0], ALU.subtract).then_inc(pool_step, 1)
                step.count[0] += 1
                bare(pool, (v_ok, 2 * B), (pool_step, POOL0 + n * MSTEPS + step.count[0]))
                step(nc.gpsimd.tensor_copy(mparts[:, 1], mrest[:, 0]))
                nc.gpsimd.tensor_tensor(mparts[:, 2], mrest[:, 0], mparts[:, 1], ALU.subtract).then_inc(mparts_ready, 1)
                assert step.count[0] == MSTEPS

            POOL0 = 4 + SLOTS - 1
            for j in range(SLOTS):
                unit(j, j)
            with pool.Fori(1, QUADS) as q:
                for j in range(SLOTS):
                    unit(q * SLOTS + j, j)

            with pool.Fori(0, B) as b:
                pool.wait_ge(u_ok, b + 1)
                nc.gpsimd.tensor_tensor(X[:, bass.ds(b * TPB, TPB)], X[:, bass.ds(b * TPB, TPB)],
                                        U2[:, bass.ds(b * TPB, TPB)], ALU.add).then_inc(res_ok, 1)

            pool.wait_ge(zeroed, 16 * SORTED)
            pool.wait_ge(slots_ok, 2)
            for t in range(T):
                pool.indirect_dma_start(sorted_x, bass.IndirectOffsetOnAxis(slot_i[:, t:t + 1], 0),
                                        XN[:, t], None).then_inc(scattered, 16)

            def expert(n, i):
                bare(pool, (slots_ok, 2), (f_ps, n - 1))
                e = pool.value_load(tile_e[0:1, bass.ds(n, 1)], min_val=0, max_val=E - 1)
                nc.gpsimd.tensor_copy(gbr[:, i], gbT[:].rearrange("p (k e) -> p k e", k=2)[:, :, bass.ds(e, 1)]
                                      .rearrange("p k a -> p (k a)"))
                nc.gpsimd.tensor_copy(w1r[:, i], w1_s[:, bass.ds(e * F, F)])
                nc.gpsimd.tensor_copy(b1r[:, i], b1T[:, bass.ds(e * FC, FC)])
                nc.gpsimd.tensor_copy(b2r[:, i], b2_s[:, bass.ds(e * D, D)])
                nc.gpsimd.tensor_copy(w2r[:, i], w2_s[:, bass.ds(e * F, F)]).then_inc(ring_ok, 1)

            pool.wait_ge(table_out, TABLES)
            pool.wait_ge(ffn_in, 16 * FFN_LOADS)
            expert(0, 0)
            expert(1, 1)
            expert(2, 0)
            with pool.Fori(0, (SORTED - 3) // 2) as r:
                expert(r * 2 + 3, 1)
                expert(r * 2 + 4, 0)

            for i in range(2):
                pool.wait_ge(ys_out[i], 16 * ((SORTED + 1 - i) // 2))
            for t in range(T):
                pool.indirect_dma_start(yg[:, t], None, sorted_y,
                                        bass.IndirectOffsetOnAxis(slot_i[:, t:t + 1], 0)).then_inc(gathered, 16)

        @block.scalar
        def _(act):
            act.wait_ge(w_in, 16 * W_LOADS)
            def batch(b):
                act.wait_ge(var_ok, b + 1)
                nc.scalar.activation(root[:], vpe[:], ACT.Sqrt).then_inc(root_ok, 1)
                for c in range(2):
                    act.wait_ge(xnT_ps, 2 * b + c + 1)
                    nc.scalar.activation(xnT[:, c * HALF:(c + 1) * HALF], SC[c][:], ACT.Copy).then_inc(xnT_sb, 1)
                for i, bias in enumerate((bq_s, bk_s)):
                    act.wait_ge(qk_ps, 2 * b + i + 1)
                    ge(act, part3, 2 * b)
                    ge(act, rows_out, b * (16 * (PARTS + 1)))
                    nc.scalar.activation(full[:, i], ST[i][:], ACT.Identity, bias=bias[:]).then_inc(full_ok, 1)
                    act.wait_ge(full_ok, 2 * b + i + 1)
                    nc.scalar.activation(parts[:, i, 0], full[:, i], ACT.Copy).then_inc(part1, 1)
                for c, bank in enumerate((OB, MB)):
                    act.wait_ge(v_ps, 2 * b + c + 1)
                    nc.scalar.activation(
                        Vall[:, bass.ds(b * (H * TPB * DK), H * TPB * DK)]
                        .rearrange("p (h t d) -> p h t d", h=H, t=TPB)[:, :, 4 * c:4 * c + 4, :]
                        .rearrange("p h t d -> p t h d"),
                        bank[:].rearrange("p (t h d) -> p t h d", t=4, h=H), ACT.Copy).then_inc(v_ok, 1)

            batch(0)
            with act.Fori(1, B) as b:
                batch(b)

            def exp_tile(u, i):
                act.wait_ge(st_written, u * TPB + i + 1)
                ge(act, pv_done, u * TPB + i - 1)
                nc.scalar.activation(probs[:, i % 2], ST[i % 2][:], ACT.Exp, scale=SCALE).then_inc(p_ready, 1)

            def take_o(pair):
                act.wait_ge(pv_done, (pair + 1) * (2 * TPB))
                ge(act, o_transposed, pair)
                nc.scalar.activation(O_s[:], OB[:, 0:QUART], ACT.Copy).then_inc(o_copied, 1)

            def slot(q, j):
                u = q * SLOTS + j
                exp_tile(u, 0)
                if j % 2 == 0 and not (isinstance(u, int) and u == 0):
                    take_o(q * 2 + j // 2 - 1)
                for i in range(1, TPB):
                    exp_tile(u, i)

            for j in range(SLOTS):
                slot(0, j)
            with act.Fori(1, QUADS) as q:
                for j in range(SLOTS):
                    slot(q, j)
            take_o(NPAIR - 1)

            with act.Fori(0, B) as b:
                for c in range(2):
                    act.wait_ge(a_ps, 2 * b + c + 1)
                    nc.scalar.activation(xnT[:, c * HALF:(c + 1) * HALF], SC[c][:], ACT.Copy).then_inc(a_sb, 1)
                act.wait_ge(var_ok, B + b * 2 + 1)
                nc.scalar.activation(root[:], vpe[:], ACT.Sqrt).then_inc(root_ok, 1)
                for c in range(2):
                    act.wait_ge(u_ps, 2 * b + c + 1)
                    nc.scalar.activation(xnT[:, c * HALF:(c + 1) * HALF], SC[c][:], ACT.Copy).then_inc(u_sb, 1)
                act.wait_ge(var_ok, B + b * 2 + 2)
                nc.scalar.activation(root[:], vpe[:], ACT.Sqrt).then_inc(root_ok, 1)
                act.wait_ge(aff_ps, b + 1)
                nc.scalar.activation(aff[:, bass.ds(b * TPB, TPB)],
                                     MB[:, 0:TPB * E].rearrange("p (t e) -> p t e", e=E), ACT.Copy).then_inc(aff_ok, 1)
            act.wait_ge(gate_ok, 1)
            nc.scalar.activation(alpha[:], top[:], ACT.Sigmoid).then_inc(act_step, 1)

            def tile(n, i):
                act.wait_ge(xs_ps, n + 1)
                act.wait_ge(ring_ok, n + 1)
                ge(act, h_ps, n - 1)
                nc.scalar.activation(xsT[:, i], SC[i][:, 0:P], ACT.Identity, bias=gbr[:, i, 1:2],
                                     scale=gbr[:, i, 0:1]).then_inc(xs_sb, 1)
                act.wait_ge(h_ps, n + 1)
                ge(act, f_ps, n - 1)
                for c in range(2):
                    nc.scalar.activation(hT[:, i, c * P:(c + 1) * P], ST[i][:, c * P:(c + 1) * P], ACT.Relu,
                                         bias=b1r[:, i, c:c + 1]).then_inc(h_act, 1)

            tile(0, 0)
            tile(1, 1)
            tile(2, 0)
            with act.Fori(0, (SORTED - 3) // 2) as r:
                tile(r * 2 + 3, 1)
                tile(r * 2 + 4, 0)

        @block.vector
        def _(dve):
            LN_STEPS = 8

            def norm(src, dst, base, nth):
                step = chain(dve, dve_step, base)
                for t in range(TPB):
                    last = nc.vector.bn_stats(stats[:, t], src(t))
                last.then_inc(dve_step, 1)
                step.count[0] += 1
                bare(dve, (x_in, 16), (dve_step, base + step.count[0]))
                for t in range(TPB):
                    last = nc.vector.bn_aggr(mv[:, t], stats[:, t])
                step(last)
                nc.vector.tensor_scalar(vpe[:], mv[:, :, 1], EPS, None, ALU.add).then_inc(var_ok, 1)
                dve.wait_ge(root_ok, nth + 1)
                step(nc.vector.reciprocal(rstd[:], root[:]))
                step(nc.vector.tensor_tensor(newt[:], rstd[:], rstd[:], ALU.mult))
                step(nc.vector.tensor_tensor(newt[:], newt[:], vpe[:], ALU.mult))
                step(nc.vector.tensor_scalar(newt[:], newt[:], -0.5, 1.5, ALU.mult, ALU.add))
                step(nc.vector.tensor_tensor(rstd[:], rstd[:], newt[:], ALU.mult))
                for t in range(TPB):
                    last = nc.vector.tensor_scalar(dst(t), src(t), mv[:, t, 0:1], rstd[:, t:t + 1], ALU.subtract, ALU.mult)
                step(last)
                assert step.count[0] == LN_STEPS

            def tile_of(tensor, b, t):
                return tensor[:, bass.ds(b * TPB + t, 1)].rearrange("p a d -> p (a d)")

            nc.vector.memset(KA[64:SROWS], 1.0).then_inc(consts, 1)

            dve.wait_ge(x_in, 16)
            def batch(b):
                bare(dve, (x_in, 16), (xnT_ps, 2 * b))
                norm(lambda t: tile_of(X, b, t), lambda t: XN[:, t], b * LN_STEPS, b)
                nc.vector.tensor_copy(newt[:], rstd[:]).then_inc(normed, 1)
                for i in range(2):
                    dve.wait_ge(rest1, 2 * b + i + 1)
                    nc.vector.tensor_copy(parts[:, i, 1], rest[:, i]).then_inc(part2, 1)

            batch(0)
            with dve.Fori(1, B) as b:
                batch(b)

            dve.wait_ge(table_T, TABLES)
            nc.vector.tensor_copy(centT[:], OB[:, 0:E]).then_inc(table_out, 1)
            nc.vector.tensor_copy(gbT[:], OB[:, 64:64 + 2 * E]).then_inc(table_out, 1)
            nc.vector.tensor_copy(b1T[:], OB[:, 128:128 + E * FC]).then_inc(table_out, 1)

            def max_tile(n, i, j):
                for c in range(2):
                    dve.wait_ge(s_written, n * (2 * TPB) + 2 * i + c + 1)
                    nc.vector.tensor_reduce(max2[:, j % 2, i, c:c + 1], SC[c][:], axis=AX.X, op=ALU.max).then_inc(s_read, 1)

            def max_end(n, j):
                dve.wait_ge(s_read, (n + 1) * (2 * TPB))
                ge(dve, mparts_ready, n)
                nc.vector.tensor_reduce(negmax[:], max2[:, j % 2], axis=AX.X, op=ALU.max, negate=True).then_inc(max_ready, 1)

            def take_shift(n, q, j):
                dve.wait_ge(mT_written, n + 1)
                ge(dve, shift_loaded[j], q * (16 * PARTS))
                nc.vector.tensor_copy(shiftT[:, j], MT).then_inc(mT_copied, 1)

            def norm_o(pair):
                dve.wait_ge(o_transposed, pair + 1)
                v = MB[:, 0:2 * P].rearrange("p (t r) -> p t r", r=VC)
                nc.vector.reciprocal(rec[:], v[:, :, 2 * DK:2 * DK + 2]).then_inc(o_rec, 1)
                dve.wait_ge(o_rec, pair + 1)
                cols = A[:].rearrange("p (b t) c -> p b t c", b=B)[
                    :, bass.ds(pair // (H // 2), 1), :, bass.ds(pair % (H // 2) * (2 * DK), 2 * DK)]
                nc.vector.tensor_tensor(
                    cols.rearrange("p a t (h d) -> p (a t) h d", h=2),
                    v[:, :, 0:2 * DK].rearrange("p t (h d) -> p t h d", h=2),
                    rec[:].unsqueeze(3).to_broadcast([P, TPB, 2, DK]), ALU.mult).then_inc(o_normed, 1)

            def slot(q, j, last=False):
                u = q * SLOTS + j
                ahead = not (last and j >= 2)
                for i in range(TPB):
                    if ahead:
                        max_tile(u + 2, i, j)
                    if i == 4 and not (last and j == SLOTS - 1):
                        take_shift(u + 1, q + (j + 1) // SLOTS, (j + 1) % SLOTS)
                    if i == 5 and j % 2 == 0 and not (isinstance(u, int) and u == 0):
                        norm_o(q * 2 + j // 2 - 1)
                if ahead:
                    max_end(u + 2, j)

            for i in range(TPB):
                max_tile(0, i, 0)
            max_end(0, 0)
            for i in range(TPB):
                max_tile(1, i, 1)
                if i == 3:
                    take_shift(0, 0, 0)
            max_end(1, 1)
            for j in range(SLOTS):
                slot(0, j)
            with dve.Fori(1, QUADS - 1) as q:
                for j in range(SLOTS):
                    slot(q, j)
            for j in range(SLOTS):
                slot(QUADS - 1, j, last=True)
            norm_o(NPAIR - 1)

            base1 = B * LN_STEPS
            with dve.Fori(0, B) as b:
                for c, bank in enumerate((OB, MB)):
                    dve.wait_ge(y_ps, 2 * b + c + 1)
                    xb = X[:, bass.ds(b * TPB + 4 * c, 4)].rearrange("p t d -> p (t d)")
                    nc.vector.tensor_tensor(xb, xb, bank[:], ALU.add).then_inc(x1_ok, 1)
                bare(dve, (x_in, 16), (x1_ok, 2 * b + 2))
                norm(lambda t: tile_of(X, b, t), lambda t: tile_of(U2, b, t), base1 + b * (2 * LN_STEPS), B + b * 2)
                nc.vector.tensor_copy(newt[:], rstd[:]).then_inc(u_ok, 1)
                norm(lambda t: tile_of(U2, b, t), lambda t: tile_of(XN, b, t), base1 + b * (2 * LN_STEPS) + LN_STEPS,
                     B + b * 2 + 1)

            step = chain(dve, dve_step, base1 + B * 2 * LN_STEPS)
            dve.wait_ge(aff_ok, B)
            step(nc.vector.tensor_reduce(top[:], aff[:], axis=AX.X, op=ALU.max))
            nc.vector.tensor_tensor(eq[:], aff[:], top[:].unsqueeze(2).to_broadcast([P, T, E]), ALU.is_ge).then_inc(gate_ok, 1)
            dve.wait_ge(gate_ok, 1)
            step(nc.vector.tensor_tensor(eq[:], eq[:], first_w[:].unsqueeze(1).to_broadcast([P, T, E]), ALU.mult))
            step(nc.vector.tensor_reduce(pick[:], eq[:], axis=AX.X, op=ALU.max))
            step(nc.vector.tensor_tensor(hot[:], eq[:], pick[:].unsqueeze(2).to_broadcast([P, T, E]), ALU.is_equal))
            nc.vector.tensor_copy(hotb[:], hot[:]).then_inc(hot_ok, 1)
            dve.wait_ge(rank_ps, 1)
            step(nc.vector.tensor_copy(tot[:], SC[1][:, 0:T * E].rearrange("p (t e) -> p e t", e=E)))
            flat = "p e t -> p (e t)"
            step(nc.vector.tensor_tensor_scan(cum[:].rearrange(flat), tot[:].rearrange(flat), zrow[:], 0.0, ALU.add, ALU.add))
            step(nc.vector.tensor_tensor(cum[:], cum[:], tot[:], ALU.subtract))
            step(nc.vector.tensor_reduce(cnt[:], tot[:], axis=AX.X, op=ALU.add))
            step(nc.vector.tensor_scalar(cnt[:], cnt[:], float(P - 1), None, ALU.add))
            step(nc.vector.tensor_copy(cnti[:], cnt[:]))
            step(nc.vector.tensor_scalar(cnti[:], cnti[:], 7, 7, ALU.logical_shift_right, ALU.logical_shift_left))
            step(nc.vector.tensor_copy(padded[:], cnti[:]))
            step(nc.vector.tensor_tensor_scan(ends[:], padded[:], zrow[:, 0:E], 0.0, ALU.add, ALU.add))
            step(nc.vector.tensor_tensor(start[:], ends[:], padded[:], ALU.subtract))
            step(nc.vector.tensor_tensor(cstart[:], start[:], cum[:, :, 0], ALU.subtract))
            step(nc.vector.tensor_tensor(cum[:], cum[:], cstart[:].unsqueeze(2).to_broadcast([P, E, T]), ALU.add))
            step(nc.vector.tensor_tensor(place[:], SC[0][:, 0:T * E].rearrange("p (t e) -> p t e", e=E),
                                         cum[:].rearrange("p e t -> p t e"), ALU.add))
            step(nc.vector.tensor_tensor(place[:], place[:], hot[:], ALU.mult))
            step(nc.vector.tensor_reduce(slot_f[:], place[:], axis=AX.X, op=ALU.add))
            nc.vector.tensor_copy(slot_i[:], slot_f[:]).then_inc(slots_ok, 1)
            step(nc.vector.tensor_tensor(tile_cmp[:], tile_at[:].unsqueeze(2).to_broadcast([P, SORTED, E]),
                                         start[:].unsqueeze(1).to_broadcast([P, SORTED, E]), ALU.is_ge))
            step(nc.vector.tensor_reduce(tile_ef[:], tile_cmp[:], axis=AX.X, op=ALU.add))
            step(nc.vector.tensor_scalar(tile_ef[:], tile_ef[:], -1.0, None, ALU.add))
            nc.vector.tensor_copy(tile_e[:], tile_ef[:]).then_inc(slots_ok, 1)

            def tile(n, i):
                dve.wait_ge(h_ps, n + 1)
                dve.wait_ge(ring_ok, n + 1)
                ge(dve, f_ps, n - 1)
                for c in range(2, FC):
                    nc.vector.tensor_scalar(hT[:, i, c * P:(c + 1) * P], ST[i][:, HALF + (c - 2) * P:HALF + (c - 1) * P],
                                            b1r[:, i, c:c + 1], 0.0, ALU.add, ALU.max).then_inc(h_dve, 1)

            def take_f(n, i, sent):
                dve.wait_ge(f_ps, n + 1)
                ge(dve, ys_out[i], sent)
                nc.vector.tensor_copy(ys[:, i], (OB, MB)[i][:, 0:D]).then_inc(f_sb, 1)

            tile(0, 0)
            tile(1, 1)
            take_f(0, 0, 0)
            tile(2, 0)
            take_f(1, 1, 0)
            with dve.Fori(0, (SORTED - 3) // 2) as r:
                tile(r * 2 + 3, 1)
                take_f(r * 2 + 2, 0, (r + 1) * 16)
                tile(r * 2 + 4, 0)
                take_f(r * 2 + 3, 1, (r + 1) * 16)
            take_f(SORTED - 1, 0, 16 * ((SORTED - 1) // 2))

            dve.wait_ge(act_step, 1)
            dve.wait_ge(res_ok, B)
            dve.wait_ge(gathered, 16 * T)
            for b in range(B):
                for t in range(b * TPB, (b + 1) * TPB):
                    last = nc.vector.scalar_tensor_tensor(yg[:, t], yg[:, t], alpha[:, t:t + 1], X[:, t], ALU.mult, ALU.add)
                last.then_inc(final_ok, 1)

        @block.tensor
        def _(pe):
            mm = nc.tensor.matmul
            pe.wait_ge(consts, CONSTS)
            pe.wait_ge(w_in, 16 * W_LOADS)
            def batch(b):
                pe.wait_ge(normed, b + 1)
                for c in range(2):
                    ge(pe, xnT_sb, 2 * b)
                    for t in range(4):
                        last = nc.tensor.transpose(SC[c][:, t * P:(t + 1) * P], XN[:, 4 * c + t], ident[:])
                    last.then_inc(xnT_ps, 1)
                pe.wait_ge(xnT_sb, 2 * b + 2)
                for i, w in enumerate((wq_s, wk_s)):
                    ge(pe, full_ok, 2 * b)
                    for c in range(2):
                        last = mm(ST[i][:, c * HALF:(c + 1) * HALF], w[:], xnT[:, c * HALF:(c + 1) * HALF],
                                  start=True, stop=True)
                    last.then_inc(qk_ps, 1)
                for c, bank in enumerate((OB, MB)):
                    ge(pe, v_ok, 2 * b)
                    for t in range(4):
                        o = bank[:, t * P:(t + 1) * P]
                        mm(o, xnT[:, (4 * c + t) * P:(4 * c + t + 1) * P], wv_s[:], start=True, stop=False)
                        last = mm(o, ones_row[:], bv_s[:], start=False, stop=True)
                    last.then_inc(v_ps, 1)

            batch(0)
            with pe.Fori(1, B) as b:
                batch(b)

            pe.wait_ge(v_ok, 2 * B)
            pe.wait_ge(ffn_in, 16 * FFN_LOADS)
            for at, src in ((0, cent_s), (64, gb_s), (128, b1_s)):
                n = src.shape[0]
                nc.tensor.transpose(OB[:, at:at + n], src[:], ident[0:n, 0:n]).then_inc(table_T, 1)
            pe.wait_ge(table_out, TABLES)

            def scores(n, i, j):
                for c in range(2):
                    ge(pe, s_read, n * (2 * TPB) + 2 * i + c - 1)
                    mm(SC[c][:], QA[0:ROWS, j, i * P:(i + 1) * P], KA[0:ROWS, j, c * HALF:(c + 1) * HALF],
                       start=True, stop=True).then_inc(s_written, 1)

            def transpose_shift(n):
                pe.wait_ge(mparts_ready, n + 1)
                ge(pe, mT_copied, n)
                nc.tensor.transpose(MT, mparts[:].rearrange("p i t -> p (i t)"), identb[:]).then_inc(mT_written, 1)

            def scores_T(u, i, j):
                ge(pe, p_ready, u * TPB + i - 1)
                for c in range(2):
                    last = mm(ST[i % 2][:, c * HALF:(c + 1) * HALF], KA[0:SROWS, j, i * P:(i + 1) * P],
                              QA[0:SROWS, j, c * HALF:(c + 1) * HALF], start=True, stop=True)
                last.then_inc(st_written, 1)

            def weigh(u, i, j):
                pe.wait_ge(p_ready, u * TPB + i + 1)
                if i == 0:
                    pe.wait_ge(v_ready, u + 1)
                for g in range(4):
                    last = mm(OB[g * VC:(g + 1) * VC, 0:QUART], Vst[:, j, i, :],
                              probs[:, i % 2, g * QUART:(g + 1) * QUART],
                              start=(i == 0 and j % 2 == 0), stop=(i == TPB - 1 and j % 2 == 1))
                last.then_inc(pv_done, 1)

            def transpose_o(pair):
                pe.wait_ge(o_copied, pair + 1)
                ge(pe, o_normed, pair)
                for c in range(2):
                    last = nc.tensor.transpose(MB[:, c * P:(c + 1) * P], O_s[:, c * P:(c + 1) * P], ident[:])
                last.then_inc(o_transposed, 1)

            def slot(q, j, last=False):
                u = q * SLOTS + j
                first = isinstance(u, int) and u == 0
                pe.wait_ge(shift_loaded[j], (q + 1) * (16 * PARTS))
                for i in range(TPB):
                    scores_T(u, i, j)
                    if i > 0:
                        if i == 1 and j % 2 == 0:
                            ge(pe, o_copied, q * 2 + j // 2)
                        weigh(u, i - 1, j)
                    elif not first:
                        weigh(u - 1, TPB - 1, (j - 1) % SLOTS)
                    if not (last and j >= 2):
                        if i == 0:
                            pe.wait_ge(qk_loaded[(j + 2) % SLOTS], (q + (j + 2) // SLOTS + 1) * 32)
                        scores(u + 2, i, (j + 2) % SLOTS)
                    if i == 3 and not (last and j == SLOTS - 1):
                        transpose_shift(u + 1)
                    if i == 4 and j % 2 == 0 and not first:
                        pe.wait_ge(mT_copied, u + 2)
                        transpose_o(q * 2 + j // 2 - 1)

            pe.wait_ge(qk_loaded[0], 32)
            for i in range(TPB):
                scores(0, i, 0)
            pe.wait_ge(qk_loaded[1], 32)
            for i in range(TPB):
                scores(1, i, 1)
                if i == 3:
                    transpose_shift(0)
            for j in range(SLOTS):
                slot(0, j)
            with pe.Fori(1, QUADS - 1) as q:
                for j in range(SLOTS):
                    slot(q, j)
            for j in range(SLOTS):
                slot(QUADS - 1, j, last=True)
            weigh(NU - 1, TPB - 1, SLOTS - 1)
            transpose_o(NPAIR - 1)

            pe.wait_ge(o_normed, NPAIR)
            for b in range(B):
                for c in range(2):
                    ge(pe, u_sb, 2 * b)
                    for t in range(4):
                        qt = 4 * c + t
                        last = nc.tensor.matmul(SC[c][:, t * P:(t + 1) * P], A[:, b * TPB + (qt % 2) * 4 + qt // 2], ident[:],
                                                is_transpose=True, start=True, stop=True)
                    last.then_inc(a_ps, 1)
                ge(pe, aff_ok, b)
                ge(pe, x1_ok, 2 * b)
                pe.wait_ge(a_sb, 2 * b + 2)
                for c, bank in enumerate((OB, MB)):
                    for t in range(4):
                        o = bank[:, t * P:(t + 1) * P]
                        mm(o, xnT[:, (4 * c + t) * P:(4 * c + t + 1) * P], wo_s[:], start=True, stop=False)
                        last = mm(o, ones_row[:], bo_s[:], start=False, stop=True)
                    last.then_inc(y_ps, 1)
                pe.wait_ge(u_ok, b + 1)
                for c in range(2):
                    for t in range(4):
                        last = nc.tensor.transpose(SC[c][:, t * P:(t + 1) * P], U2[:, b * TPB + 4 * c + t], ident[:])
                    last.then_inc(u_ps, 1)
                pe.wait_ge(u_sb, 2 * b + 2)
                for t in range(TPB):
                    last = mm(MB[:, t * E:(t + 1) * E], xnT[:, t * P:(t + 1) * P], centT[:], start=True, stop=True)
                last.then_inc(aff_ps, 1)

            pe.wait_ge(hot_ok, 1)
            mm(SC[0][:, 0:T * E], before[:], hotb[:].rearrange("p t e -> p (t e)"), start=True, stop=True)
            mm(SC[1][:, 0:T * E], onesb[:], hotb[:].rearrange("p t e -> p (t e)"), start=True, stop=True).then_inc(rank_ps, 1)
            pe.wait_ge(slots_ok, 1)

            def take_x(n, i, loaded):
                pe.wait_ge(xs_in[i], loaded)
                ge(pe, xs_sb, n - 1)
                nc.tensor.transpose(SC[i][:, 0:P], xs[:, i], ident[:]).then_inc(xs_ps, 1)

            def hidden(n, i):
                pe.wait_ge(xs_sb, n + 1)
                pe.wait_ge(ring_ok, n + 1)
                ge(pe, h_act, 2 * (n - 1))
                ge(pe, h_dve, 2 * (n - 1))
                for c in range(FC):
                    o = c * P if c < 2 else HALF + (c - 2) * P
                    last = mm(ST[i][:, o:o + P], w1r[:, i, c * P:(c + 1) * P], xsT[:, i], start=True, stop=True)
                last.then_inc(h_ps, 1)

            def project(n, i):
                pe.wait_ge(h_act, 2 * (n + 1))
                pe.wait_ge(h_dve, 2 * (n + 1))
                ge(pe, f_sb, n - 1)
                o = (OB, MB)[i][:, 0:D]
                for c in range(FC):
                    mm(o, hT[:, i, c * P:(c + 1) * P], w2r[:, i, c * D:(c + 1) * D], start=(c == 0), stop=False)
                mm(o, ones_row[:], b2r[:, i], start=False, stop=True).then_inc(f_ps, 1)

            take_x(0, 0, 16)
            hidden(0, 0)
            take_x(1, 1, 16)
            hidden(1, 1)
            project(0, 0)
            take_x(2, 0, 32)
            hidden(2, 0)
            project(1, 1)
            with pe.Fori(0, (SORTED - 3) // 2) as r:
                take_x(r * 2 + 3, 1, r * 16 + 32)
                hidden(r * 2 + 3, 1)
                project(r * 2 + 2, 0)
                take_x(r * 2 + 4, 0, r * 16 + 48)
                hidden(r * 2 + 4, 0)
                project(r * 2 + 3, 1)
            project(SORTED - 1, 0)


_INS = ['L0_attn_x', 'L0_attn_Wq', 'L0_attn_bq', 'L0_attn_Wk', 'L0_attn_bk', 'L0_attn_Wv', 'L0_attn_bv', 'L0_attn_Wo',
        'L0_attn_bo', 'L0_ffn_centroids', 'L0_ffn_ln_g', 'L0_ffn_ln_b', 'L0_ffn_w1', 'L0_ffn_b1', 'L0_ffn_w2', 'L0_ffn_b2']


def kernel(**inputs):
    import numpy as _np
    import concourse.bacc as _bacc
    from concourse import mybir as _mybir
    from concourse.bass_utils import run_bass_kernel_spmd as _run

    nc = _bacc.Bacc("TRN2", target_bir_lowering=False, num_devices=1)
    arrays, args = {}, []
    for name in _INS:
        a = _np.ascontiguousarray(inputs[name])
        arrays[f"in_{name}"] = a
        args.append(nc.dram_tensor(f"in_{name}", a.shape, _mybir.dt.from_np(a.dtype), kind="ExternalInput").ap())
    out = nc.dram_tensor("out_y", inputs["L0_attn_x"].shape, _mybir.dt.float32, kind="ExternalOutput").ap()
    build(nc, *args, out)
    r = _run(nc, [arrays], core_ids=[0])
    return r.results[0]["out_y"]
```

```python
import concourse.bass as bass
import concourse.mybir as mybir
from contextlib import ExitStack

F32 = mybir.dt.float32
BF16 = mybir.dt.bfloat16
I32 = mybir.dt.int32
ALU = mybir.AluOpType
ACT = mybir.ActivationFunctionType
AX = mybir.AxisListType

P = 128
B, S, D = 4, 1024, 128
H = 16
DK = D // H
E, F = 8, 512
EPS = 1e-5
TPB = S // P
T = B * TPB
NU = B * H
NPAIR = NU // 2
PARTS = 3
ROWS = PARTS * PARTS * DK
SHIFT = 96
SLOTS = 4
QUADS = NU // SLOTS
VC = 32
QUART = S // 4
HALF = 512
FC = F // P
SORTED = T + E - 1
FIRST_FULL = 4
FULL = (SORTED - 2 - FIRST_FULL) // 2 * 2
SHIFT_AT = 2
SCALE = float(DK) ** -0.5


def ge(eng, sem, value):
    if isinstance(value, int) and value <= 0:
        return
    eng.wait_ge(sem, value)


def bare(eng, held, *waits):
    waits = [(s, v) for s, v in waits if not (isinstance(v, int) and v <= 0)]
    waits = [(s, v if isinstance(v, int) else eng.to_reg(v)) for s, v in waits]
    eng.wait_ge(*held)
    for s, v in waits:
        eng.wait_ge(s, v)


def staged(eng, step):
    for n in range(FIRST_FULL):
        step(n, n % 2)
    with eng.Fori(0, FULL // 2) as r:
        for i in range(2):
            step(r * 2 + (FIRST_FULL + i), i)
    for n in range(FIRST_FULL + FULL, SORTED + 2):
        step(n, n % 2)


def chain(eng, sem, base=0):
    n = [0]

    def step(ins):
        n[0] += 1
        ins.then_inc(sem, 1)
        eng.wait_ge(sem, base + n[0])
    step.count = n
    return step


def build(nc, x, Wq, bq, Wk, bk, Wv, bv, Wo, bo, cent, ln_g, ln_b, w1, b1, w2, b2, out):
    ctx = ExitStack()
    with ctx:
        def sb(name, shape, dt=F32):
            return ctx.enter_context(nc.sbuf_tensor(name, shape, dt))

        def sem(name):
            return ctx.enter_context(nc.semaphore(name))

        q_parts = nc.dram_tensor("q_parts", (NU, PARTS, DK, S), BF16, kind="Internal").ap()
        k_parts = nc.dram_tensor("k_parts", (NU, DK, PARTS, S), BF16, kind="Internal").ap()
        sorted_x = nc.dram_tensor("sorted_x", (SORTED * P, D), F32, kind="Internal").ap()
        sorted_y = nc.dram_tensor("sorted_y", (SORTED * P, D), F32, kind="Internal").ap()

        wq_s, wk_s, wv_s, wo_s = (sb(n, [P, D]) for n in ("wq_s", "wk_s", "wv_s", "wo_s"))
        bq_s, bk_s = sb("bq_s", [P, 1]), sb("bk_s", [P, 1])
        bv_s, bo_s = sb("bv_s", [P, D]), sb("bo_s", [P, D])
        cent_s, centT = sb("cent_s", [E, D]), sb("centT", [P, E])
        gb_s, gbT = sb("gb_s", [2 * E, D]), sb("gbT", [P, 2 * E])
        b2_s = sb("b2_s", [P, E * D])
        w1_s, w2_s = sb("w1_s", [P, E * F]), sb("w2_s", [P, E * F])
        ident, identb = sb("ident", [P, P]), sb("identb", [P, P], BF16)
        before = sb("before", [P, P], BF16)
        onesb = sb("onesb", [P, P], BF16)
        zeros = sb("zeros", [P, D])

        X = sb("X", [P, T, D])
        Vall = sb("Vall", [P, NU * TPB * DK])
        A = sb("A", [P, T, D])
        U2 = sb("U2", [P, T, D])
        XN = sb("XN", [P, T, D])
        stats, mv = sb("stats", [P, TPB, 6]), sb("mv", [P, TPB, 2])
        rstd, vpe, root, newt = (sb(n, [P, TPB]) for n in ("rstd", "vpe", "root", "newt"))
        xnT = sb("xnT", [P, S])
        work = sb("work", [P, 4, S])
        full = [work[:, 0:2], A[:, 0:TPB * 2].rearrange("p t c -> p (t c)").rearrange("p (i s) -> p i s", i=2)]
        rest = [work[:, 2:4], A[:, TPB * 2:T].rearrange("p t c -> p (t c)").rearrange("p (i s) -> p i s", i=2)]
        parts = [sb("parts", [P, 2, PARTS, S], BF16)[:],
                 U2[:].rearrange("p t c -> p (t c)").bitcast(BF16)[:, 0:2 * PARTS * S]
                 .rearrange("p (i j s) -> p i j s", i=2, j=PARTS)]
        b1_s = work[:].rearrange("p i s -> p (i s)")
        QA, KA = sb("QA", [P, SLOTS, S], BF16), sb("KA", [P, SLOTS, S], BF16)
        Vst = sb("Vst", [P, SLOTS, TPB, VC])
        probs = sb("probs", [P, 2, S])
        max2 = sb("max2", [P, 2, TPB, 2])
        negmax, mrest = sb("negmax", [P, TPB]), sb("mrest", [P, 2, TPB])
        mparts = sb("mparts", [P, PARTS, TPB], BF16)
        shiftT = sb("shiftT", [PARTS * TPB, SLOTS, P], BF16)
        O_s = sb("O_s", [P, QUART])
        rec = sb("rec", [P, TPB, 2])
        OT_s = sb("OT_s", [P, 2, QUART])

        aff, eq = sb("aff", [P, T, E]), sb("eq", [P, T, E])
        top, alpha, pick = sb("top", [P, T]), sb("alpha", [P, T]), sb("pick", [P, T])
        first_w = sb("first_w", [P, E])
        hot, hotb = sb("hot", [P, T, E]), sb("hotb", [P, T, E], BF16)
        tot, cum = sb("tot", [P, E, T]), sb("cum", [P, E, T])
        zrow = sb("zrow", [P, E * T])
        cnt, cnti = sb("cnt", [P, E]), sb("cnti", [P, E], I32)
        padded, ends, start = sb("padded", [P, E]), sb("ends", [P, E]), sb("start", [P, E])
        cstart = sb("cstart", [P, E])
        place, slot_f, slot_i = sb("place", [P, T, E]), sb("slot_f", [P, T]), sb("slot_i", [P, T], I32)
        tile_at, tile_cmp = sb("tile_at", [P, SORTED]), sb("tile_cmp", [P, SORTED, E])
        tile_ef, tile_e = sb("tile_ef", [P, SORTED]), sb("tile_e", [P, SORTED], I32)

        xs = sb("xs", [P, 2, D])
        xsT = sb("xsT", [P, 2, P])
        hs = A[:, 0:TPB].rearrange("p (i c) d -> p i (c d)", i=2)
        hT = A[:, TPB:2 * TPB].rearrange("p (i c) d -> p i (c d)", i=2)
        ys = sb("ys", [P, 2, D])
        yg = U2

        ST = [ctx.enter_context(nc.psum_tensor(f"ST{i}", [P, S], F32)) for i in range(2)]
        SC = [ctx.enter_context(nc.psum_tensor(f"SC{i}", [P, HALF], F32)) for i in range(2)]
        OB = ctx.enter_context(nc.psum_tensor("OB", [P, HALF], F32))
        MB = ctx.enter_context(nc.psum_tensor("MB", [P, HALF], F32))
        MT = MB[0:PARTS * TPB, 2 * P:2 * P + P // 2].bitcast(BF16)

        x_in = [sem(f"x_in{b}") for b in range(B)]
        w_in, ffn_in, b1_in = sem("w_in"), sem("ffn_in"), sem("b1_in")
        consts, table_in, table_T, table_out = sem("consts"), sem("table_in"), sem("table_T"), sem("table_out")
        pool_step, dve_step, act_step = sem("pool_step"), sem("dve_step"), sem("act_step")
        var_ok, root_ok = sem("var_ok"), sem("root_ok")
        normed, xnT_ps, xnT_sb = sem("normed"), sem("xnT_ps"), sem("xnT_sb")
        qk_ps, v_ps, full_ok, v_ok = sem("qk_ps"), sem("v_ps"), sem("full_ok"), sem("v_ok")
        part1, rest1, part2, part3 = (sem(n) for n in ("part1", "rest1", "part2", "part3"))
        parts_out = [sem(f"parts_out{b}") for b in range(B)]
        bo_ok = sem("bo_ok")
        qk_loaded = [sem(f"qk_loaded{j}") for j in range(SLOTS)]
        shift_loaded = [sem(f"shift_loaded{j}") for j in range(SLOTS)]
        s_written, s_read = sem("s_written"), sem("s_read")
        st_written, p_ready, pv_done = sem("st_written"), sem("p_ready"), sem("pv_done")
        v_ready, max_ready, mparts_ready = sem("v_ready"), sem("max_ready"), sem("mparts_ready")
        mT_written, mT_copied = sem("mT_written"), sem("mT_copied")
        o_copied, o_transposed, oT_copied = (sem(n) for n in ("o_copied", "o_transposed", "oT_copied"))
        o_rec, o_normed = sem("o_rec"), sem("o_normed")
        a_ps, a_sb, y_ps, x1_ok = sem("a_ps"), sem("a_sb"), sem("y_ps"), sem("x1_ok")
        u_ok, u_ps, u_sb, aff_ps, aff_ok, xn_ok = (sem(n) for n in ("u_ok", "u_ps", "u_sb", "aff_ps", "aff_ok", "xn_ok"))
        res_ok, gate_ok, hot_ok, rank_ps, slots_ok = (sem(n) for n in ("res_ok", "gate_ok", "hot_ok", "rank_ps", "slots_ok"))
        zeroed, scattered = sem("zeroed"), sem("scattered")
        xs_in = [sem(f"xs_in{i}") for i in range(2)]
        ys_out = [sem(f"ys_out{i}") for i in range(2)]
        xs_ps, xs_sb, h_ps, h_sb, ht_ps, ht_sb, f_ps, f_sb = (
            sem(n) for n in ("xs_ps", "xs_sb", "h_ps", "h_sb", "ht_ps", "ht_sb", "f_ps", "f_sb"))
        gathered, final_ok, out_done = sem("gathered"), sem("final_ok"), sem("out_done")

        W_LOADS, FFN_LOADS, CONSTS = 8, 3, 10
        TABLES = 2
        block = ctx.enter_context(nc.Block())

        @block.sync
        def _(sp):
            def load_tokens(b):
                sp.dma_start(X[:, b * TPB:(b + 1) * TPB], x[b].rearrange("(t p) d -> p t d", p=P)).then_inc(x_in[b], 16)

            load_tokens(0)
            for dst, src in ((wq_s, Wq), (wk_s, Wk)):
                sp.dma_start(dst[:], src).then_inc(w_in, 16)
            for dst, src in ((bq_s, bq), (bk_s, bk)):
                sp.dma_start(dst[:], src.rearrange("(p a) -> p a", a=1)).then_inc(w_in, 16)
            load_tokens(1)
            for dst, src in ((wv_s, Wv), (wo_s, Wo)):
                sp.dma_start(dst[:], src).then_inc(w_in, 16)
            for dst, src in ((bv_s, bv), (bo_s, bo)):
                sp.dma_start(dst[:], src.partition_broadcast(P)).then_inc(w_in, 16)
            load_tokens(2)
            load_tokens(3)
            sp.dma_start(cent_s[:], cent).then_inc(table_in, 16)
            sp.dma_start(gb_s[0:E, :], ln_g).then_inc(table_in, 16)
            sp.dma_start(gb_s[E:2 * E, :], ln_b).then_inc(table_in, 16)

            for b in range(B):
                sp.wait_ge(part3, 2 * b + 2)
                for i in range(PARTS):
                    sp.dma_start(q_parts[b * H:(b + 1) * H, i], parts[b % 2][:, 0, i]).then_inc(parts_out[b], 16)
                sp.dma_start(k_parts[b * H:(b + 1) * H].rearrange("h d j s -> (h d) (j s)"),
                             parts[b % 2][:, 1].rearrange("p j s -> p (j s)")).then_inc(parts_out[b], 16)
            sp.wait_ge(consts, CONSTS)
            sp.wait_ge(parts_out[0], 16 * (PARTS + 1))

            def load(n, j):
                ge(sp, st_written, TPB * (n - SLOTS + 1))
                sp.dma_start(QA[0:ROWS, j],
                             q_parts[bass.ds(n, 1)].rearrange("a i d s -> (a i d) s").unsqueeze(1)
                             .to_broadcast([PARTS * DK, PARTS, S])).then_inc(qk_loaded[j], 16)
                sp.dma_start(KA[0:ROWS, j],
                             k_parts[bass.ds(n, 1)].rearrange("a d j s -> a (d j) s")
                             .to_broadcast([PARTS, DK * PARTS, S])).then_inc(qk_loaded[j], 16)

            def shift(n, j):
                sp.wait_ge(mT_copied, n + 1)
                for i in range(PARTS):
                    sp.dma_start(QA[SHIFT + i:SHIFT + i + 1, j, :].rearrange("a (t q) -> a t q", t=TPB),
                                 shiftT[TPB * i:TPB * (i + 1), j, :]).then_inc(shift_loaded[j], 16)

            for n in range(SLOTS):
                load(n, n)
            for b in range(1, B):
                sp.wait_ge(parts_out[b], 16 * (PARTS + 1))
            sp.dma_start(w1_s[:].rearrange("p (e f) -> p e f", e=E), w1.rearrange("e p f -> p e f")).then_inc(ffn_in, 16)
            sp.dma_start(w2_s[:].rearrange("p (e c d) -> p e c d", e=E, c=FC),
                         w2.rearrange("e (c p) d -> p e c d", p=P)).then_inc(ffn_in, 16)
            sp.dma_start(b2_s[:], b2.rearrange("e d -> (e d)").partition_broadcast(P)).then_inc(ffn_in, 16)
            sp.dma_start(b1_s, b1.rearrange("e f -> (e f)").partition_broadcast(P)).then_inc(b1_in, 16)
            shift(0, 0)

            def slot(u, j, last=False):
                if not (last and j > 0) and not (isinstance(u, int) and u == 0):
                    load(u + 3, (j + 3) % SLOTS)
                if not (last and j == SLOTS - 1):
                    shift(u + 1, (j + 1) % SLOTS)

            for j in range(SLOTS):
                slot(j, j)
            with sp.Fori(1, QUADS - 1) as q:
                for j in range(SLOTS):
                    slot(q * SLOTS + j, j)
            for j in range(SLOTS):
                slot(NU - SLOTS + j, j, last=True)

            sp.wait_ge(scattered, 16 * T)

            def load_x(n, i):
                ge(sp, xs_ps, n - 1)
                sp.dma_start(xs[:, i], sorted_x[bass.ds(n * P, P), :]).then_inc(xs_in[i], 16)

            def store_y(n, i):
                sp.wait_ge(f_sb, n + 1)
                sp.dma_start(sorted_y[bass.ds(n * P, P), :], ys[:, i]).then_inc(ys_out[i], 16)

            def step(n, i):
                if not isinstance(n, int) or n + 2 < SORTED:
                    load_x(n + 2, i)
                if not isinstance(n, int) or n >= 2:
                    store_y(n - 2, i)

            load_x(0, 0)
            load_x(1, 1)
            staged(sp, step)

            for b in range(B):
                sp.wait_ge(final_ok, b + 1)
                sp.dma_start(out[b].rearrange("(t p) d -> p t d", p=P), yg[:, b * TPB:(b + 1) * TPB]).then_inc(out_done, 16)
            sp.wait_ge(out_done, 16 * B)
            for i in range(2):
                sp.wait_ge(ys_out[i], 16 * ((SORTED + 1 - i) // 2))
            sp.wait_ge(zeroed, 16 * SORTED)

        @block.gpsimd
        def _(pool):
            nc.gpsimd.memset(ident[:], 0.0).then_inc(pool_step, 1)
            nc.gpsimd.memset(identb[:], 0.0).then_inc(pool_step, 1)
            nc.gpsimd.memset(before[:], 1.0).then_inc(pool_step, 1)
            nc.gpsimd.memset(Vst[:], 0.0).then_inc(pool_step, 1)
            nc.gpsimd.memset(zeros[:], 0.0).then_inc(pool_step, 1)
            nc.gpsimd.memset(onesb[:], 1.0).then_inc(consts, 1)
            nc.gpsimd.memset(zrow[:], 0.0).then_inc(consts, 1)
            nc.gpsimd.iota(first_w[:], [[-1, E]], base=E, channel_multiplier=0,
                           allow_small_or_imprecise_dtypes=True).then_inc(consts, 1)
            nc.gpsimd.iota(tile_at[:], [[P, SORTED]], base=0, channel_multiplier=0,
                           allow_small_or_imprecise_dtypes=True).then_inc(consts, 1)
            pool.wait_ge(pool_step, 5)
            for m in (ident, identb):
                nc.gpsimd.affine_select(out=m[:], in_=m[:], compare_op=ALU.not_equal, fill=1.0, base=0,
                                        pattern=[[-1, P]], channel_multiplier=1).then_inc(consts, 1)
            nc.gpsimd.affine_select(out=before[:], in_=before[:], compare_op=ALU.is_gt, fill=0.0, base=0,
                                    pattern=[[1, P]], channel_multiplier=-1).then_inc(consts, 1)
            for j in range(SLOTS):
                last = nc.gpsimd.memset(Vst[:, j, :, 2 * DK + j % 2:2 * DK + j % 2 + 1], 1.0)
                last.then_inc(consts if j == SLOTS - 1 else pool_step, 1)

            for n in range(SORTED):
                pool.dma_start(sorted_x[n * P:(n + 1) * P, :], zeros[:]).then_inc(zeroed, 16)

            pool.wait_ge(v_ok, 2 * B)

            pool.wait_ge(part3, 2 * B)
            MSTEPS = 3

            def norm_o(pair, r):
                pool.wait_ge(o_rec, pair + 1)
                v = OT_s[:, r].rearrange("p (t c) -> p t c", c=VC)
                cols = A[:].rearrange("p (b t) c -> p b t c", b=B)[
                    :, bass.ds(pair // (H // 2), 1), :, bass.ds(pair % (H // 2) * (2 * DK), 2 * DK)]
                nc.gpsimd.tensor_tensor(
                    cols.rearrange("p a t (h d) -> p (a t) h d", h=2),
                    v[:, :, 0:2 * DK].rearrange("p t (h d) -> p t h d", h=2),
                    rec[:].unsqueeze(3).to_broadcast([P, TPB, 2, DK]), ALU.mult).then_inc(o_normed, 1)

            def unit(n, j, pair=None):
                bare(pool, (v_ok, 2 * B), (pv_done, TPB * (n - SLOTS + 1)))
                nc.gpsimd.tensor_copy(Vst[:, j, :, (j % 2) * DK:(j % 2 + 1) * DK],
                                      Vall[:, bass.ds(n * (TPB * DK), TPB * DK)].rearrange("p (t d) -> p t d", d=DK)
                                      ).then_inc(v_ready, 1)
                if j % 2 == 0 and pair is not None:
                    norm_o(pair, j // 2)
                bare(pool, (v_ok, 2 * B), (max_ready, n + 1), (mT_written, n))
                step = chain(pool, pool_step, POOL0 + n * MSTEPS)
                step(nc.gpsimd.tensor_copy(mparts[:, 0], negmax[:]))
                nc.gpsimd.tensor_tensor(mrest[:, 0], negmax[:], mparts[:, 0], ALU.subtract).then_inc(pool_step, 1)
                step.count[0] += 1
                bare(pool, (v_ok, 2 * B), (pool_step, POOL0 + n * MSTEPS + step.count[0]))
                step(nc.gpsimd.tensor_copy(mparts[:, 1], mrest[:, 0]))
                nc.gpsimd.tensor_tensor(mparts[:, 2], mrest[:, 0], mparts[:, 1], ALU.subtract).then_inc(mparts_ready, 1)
                assert step.count[0] == MSTEPS

            POOL0 = 5 + SLOTS - 1
            for j in range(SLOTS):
                unit(j, j)
                nc.gpsimd.tensor_tensor(X[:, j * TPB:(j + 1) * TPB], X[:, j * TPB:(j + 1) * TPB],
                                        bo_s[:].unsqueeze(1).to_broadcast([P, TPB, D]), ALU.add).then_inc(bo_ok, 1)
            assert SLOTS == B
            with pool.Fori(1, QUADS) as q:
                for j in range(SLOTS):
                    unit(q * SLOTS + j, j, pair=q * 2 + (j // 2 - 2))
            norm_o(NPAIR - 2, 0)
            norm_o(NPAIR - 1, 1)

            with pool.Fori(0, B) as b:
                pool.wait_ge(u_ok, b + 1)
                nc.gpsimd.tensor_tensor(X[:, bass.ds(b * TPB, TPB)], X[:, bass.ds(b * TPB, TPB)],
                                        U2[:, bass.ds(b * TPB, TPB)], ALU.add).then_inc(res_ok, 1)

            pool.wait_ge(zeroed, 16 * SORTED)
            pool.wait_ge(slots_ok, 2)
            for t in range(T):
                pool.indirect_dma_start(sorted_x, bass.IndirectOffsetOnAxis(slot_i[:, t:t + 1], 0),
                                        XN[:, t], None).then_inc(scattered, 16)

            pool.wait_ge(res_ok, B)
            for i in range(2):
                pool.wait_ge(ys_out[i], 16 * ((SORTED + 1 - i) // 2))
            for t in range(T):
                pool.indirect_dma_start(yg[:, t], None, sorted_y,
                                        bass.IndirectOffsetOnAxis(slot_i[:, t:t + 1], 0)).then_inc(gathered, 16)

        @block.scalar
        def _(act):
            act.wait_ge(w_in, 16 * W_LOADS)
            def take_root(n):
                act.wait_ge(var_ok, n + 1)
                nc.scalar.activation(root[:], vpe[:], ACT.Sqrt).then_inc(root_ok, 1)

            def take_xnT(b):
                for c in range(2):
                    act.wait_ge(xnT_ps, 2 * b + c + 1)
                    nc.scalar.activation(xnT[:, c * HALF:(c + 1) * HALF], SC[c][:], ACT.Copy).then_inc(xnT_sb, 1)

            def take_full(b):
                for i, bias in enumerate((bq_s, bk_s)):
                    act.wait_ge(qk_ps, 2 * b + i + 1)
                    if b >= 2:
                        act.wait_ge(part3, 2 * (b - 1))
                        act.wait_ge(parts_out[b - 2], 16 * (PARTS + 1))
                    nc.scalar.activation(full[b % 2][:, i], ST[i][:], ACT.Identity, bias=bias[:]).then_inc(full_ok, 1)
                for i in range(2):
                    act.wait_ge(full_ok, 2 * b + i + 1)
                    nc.scalar.activation(parts[b % 2][:, i, 0], full[b % 2][:, i], ACT.Copy).then_inc(part1, 1)

            def take_part2(b):
                for i in range(2):
                    act.wait_ge(rest1, 2 * b + i + 1)
                    nc.scalar.activation(parts[b % 2][:, i, 1], rest[b % 2][:, i], ACT.Copy).then_inc(part2, 1)

            take_root(0)
            take_root(1)
            for b in range(B):
                take_xnT(b)
                if b > 0:
                    take_part2(b - 1)
                take_full(b)
                if b + 2 < B:
                    take_root(b + 2)
            take_part2(B - 1)

            def exp_tile(u, i):
                act.wait_ge(st_written, u * TPB + i + 1)
                ge(act, pv_done, u * TPB + i - 1)
                nc.scalar.activation(probs[:, i % 2], ST[i % 2][:], ACT.Exp, scale=SCALE).then_inc(p_ready, 1)

            def take_o(pair):
                act.wait_ge(pv_done, (pair + 1) * (2 * TPB))
                ge(act, o_transposed, pair)
                nc.scalar.activation(O_s[:], OB[:, 0:QUART], ACT.Copy).then_inc(o_copied, 1)

            def take_shift(n, q, j):
                act.wait_ge(mT_written, n + 1)
                ge(act, shift_loaded[j], q * (16 * PARTS))
                nc.scalar.activation(shiftT[:, j], MT, ACT.Copy).then_inc(mT_copied, 1)

            def take_oT(pair, r):
                act.wait_ge(o_transposed, pair + 1)
                ge(act, o_normed, pair - 1)
                nc.scalar.activation(OT_s[:, r], MB[:, 0:QUART], ACT.Copy).then_inc(oT_copied, 1)

            def slot(q, j, last=False):
                u = q * SLOTS + j
                pair = q * 2 + j // 2 - 1
                for i in range(TPB):
                    exp_tile(u, i)
                    if i == 0 and j % 2 == 0 and not (isinstance(u, int) and u == 0):
                        take_o(pair)
                    if i == SHIFT_AT + 1 and not (last and j == SLOTS - 1):
                        take_shift(u + 1, q + (j + 1) // SLOTS, (j + 1) % SLOTS)
                    if i == SHIFT_AT + 3 and j % 2 == 0 and not (isinstance(u, int) and u == 0):
                        take_oT(pair, (j // 2 + 1) % 2)

            take_shift(0, 0, 0)
            for j in range(SLOTS):
                slot(0, j)
            with act.Fori(1, QUADS - 1) as q:
                for j in range(SLOTS):
                    slot(q, j)
            for j in range(SLOTS):
                slot(QUADS - 1, j, last=True)
            take_o(NPAIR - 1)
            take_oT(NPAIR - 1, 1)

            def take_aT(b):
                for c in range(2):
                    act.wait_ge(a_ps, 2 * b + c + 1)
                    nc.scalar.activation(xnT[:, c * HALF:(c + 1) * HALF], SC[c][:], ACT.Copy).then_inc(a_sb, 1)

            def take_uT(b):
                for c, bank in enumerate((OB, MB)):
                    act.wait_ge(u_ps, 2 * b + c + 1)
                    nc.scalar.activation(probs[:, 0, c * HALF:(c + 1) * HALF], bank[:], ACT.Copy).then_inc(u_sb, 1)

            def take_aff(b):
                act.wait_ge(aff_ps, b + 1)
                nc.scalar.activation(aff[:, b * TPB:(b + 1) * TPB],
                                     OB[:, 0:TPB * E].rearrange("p (t e) -> p t e", e=E), ACT.Copy).then_inc(aff_ok, 1)

            take_aT(0)
            for b in range(B):
                if b + 1 < B:
                    take_aT(b + 1)
                take_root(B + 2 * b)
                take_root(B + 2 * b + 1)
                take_uT(b)
                take_aff(b)
            act.wait_ge(gate_ok, 1)
            nc.scalar.activation(alpha[:], top[:], ACT.Sigmoid).then_inc(act_step, 1)

            act.wait_ge(table_out, TABLES)
            act.wait_ge(slots_ok, 2)

            def gain(n, i):
                e = act.value_load(tile_e[0:1, bass.ds(n, 1)], min_val=0, max_val=E - 1)
                act.wait_ge(xs_ps, n + 1)
                ge(act, h_ps, n - 1)
                nc.scalar.activation(xsT[:, i], SC[i][:, 0:P], ACT.Identity, bias=gbT[:, bass.ds(e + E, 1)],
                                     scale=gbT[:, bass.ds(e, 1)]).then_inc(xs_sb, 1)

            def relu(n, i):
                act.wait_ge(ht_ps, n + 1)
                ge(act, f_ps, n - 1)
                nc.scalar.activation(hT[:, i], ST[i][:, HALF:S], ACT.Relu).then_inc(ht_sb, 1)

            def step(n, i):
                if not isinstance(n, int) or n + 1 < SORTED:
                    gain(n + 1, 1 - i)
                if not isinstance(n, int) or 0 <= n - 1 < SORTED:
                    relu(n - 1, 1 - i)

            gain(0, 0)
            staged(act, step)

        @block.vector
        def _(dve):
            LN_STEPS = 8

            def norm(src, dst, base, nth):
                step = chain(dve, dve_step, base)
                for t in range(TPB):
                    last = nc.vector.bn_stats(stats[:, t], src(t))
                last.then_inc(dve_step, 1)
                step.count[0] += 1
                dve.wait_ge(dve_step, base + step.count[0])
                for t in range(TPB):
                    last = nc.vector.bn_aggr(mv[:, t], stats[:, t])
                step(last)
                nc.vector.tensor_scalar(vpe[:], mv[:, :, 1], EPS, None, ALU.add).then_inc(var_ok, 1)
                dve.wait_ge(root_ok, nth + 1)
                step(nc.vector.reciprocal(rstd[:], root[:]))
                step(nc.vector.tensor_tensor(newt[:], rstd[:], rstd[:], ALU.mult))
                step(nc.vector.tensor_tensor(newt[:], newt[:], vpe[:], ALU.mult))
                step(nc.vector.tensor_scalar(newt[:], newt[:], -0.5, 1.5, ALU.mult, ALU.add))
                step(nc.vector.tensor_tensor(rstd[:], rstd[:], newt[:], ALU.mult))
                for t in range(TPB):
                    last = nc.vector.tensor_scalar(dst(t), src(t), mv[:, t, 0:1], rstd[:, t:t + 1], ALU.subtract, ALU.mult)
                step(last)
                assert step.count[0] == LN_STEPS

            def tile_of(tensor, b, t):
                return tensor[:, bass.ds(b * TPB + t, 1)].rearrange("p a d -> p (a d)")

            nc.vector.memset(KA[64:P], 1.0).then_inc(consts, 1)
            nc.vector.memset(QA[64:P], 0.0).then_inc(consts, 1)

            def norm_x(b):
                dve.wait_ge(x_in[b], 16)
                ge(dve, xnT_ps, 2 * (b - 1))
                r = b % 2 * TPB
                norm(lambda t: X[:, b * TPB + t], lambda t: XN[:, r + t], b * LN_STEPS, b)
                nc.vector.tensor_copy(newt[:], rstd[:]).then_inc(normed, 1)

            def take_values(b):
                for c, bank in enumerate((OB, MB)):
                    dve.wait_ge(v_ps, 2 * b + c + 1)
                    nc.vector.tensor_tensor(
                        Vall[:, b * (H * TPB * DK):(b + 1) * (H * TPB * DK)]
                        .rearrange("p (h t d) -> p h t d", h=H, t=TPB)[:, :, 4 * c:4 * c + 4, :]
                        .rearrange("p h t d -> p t h d"),
                        bank[:].rearrange("p (t h d) -> p t h d", t=4, h=H),
                        bv_s[:].rearrange("p (h d) -> p h d", h=H).unsqueeze(1).to_broadcast([P, 4, H, DK]),
                        ALU.add).then_inc(v_ok, 1)

            def take_rest(b):
                for i in range(2):
                    dve.wait_ge(part1, 2 * b + i + 1)
                    nc.vector.tensor_tensor(rest[b % 2][:, i], full[b % 2][:, i], parts[b % 2][:, i, 0],
                                            ALU.subtract).then_inc(rest1, 1)

            def take_part3(b):
                for i in range(2):
                    dve.wait_ge(part2, 2 * b + i + 1)
                    nc.vector.tensor_tensor(parts[b % 2][:, i, 2], rest[b % 2][:, i], parts[b % 2][:, i, 1],
                                            ALU.subtract).then_inc(part3, 1)

            norm_x(0)
            norm_x(1)
            dve.wait_ge(w_in, 16 * W_LOADS)
            for b in range(B):
                take_values(b)
                take_rest(b)
                if b + 2 < B:
                    norm_x(b + 2)
                take_part3(b)

            dve.wait_ge(table_T, TABLES)
            nc.vector.tensor_copy(centT[:], OB[:, 0:E]).then_inc(table_out, 1)
            nc.vector.tensor_copy(gbT[:], OB[:, 64:64 + 2 * E]).then_inc(table_out, 1)

            def max_tile(n, i, j):
                for c in range(2):
                    dve.wait_ge(s_written, n * (2 * TPB) + 2 * i + c + 1)
                    nc.vector.tensor_reduce(max2[:, j % 2, i, c:c + 1], SC[c][:], axis=AX.X, op=ALU.max).then_inc(s_read, 1)

            def max_end(n, j):
                dve.wait_ge(s_read, (n + 1) * (2 * TPB))
                ge(dve, mparts_ready, n)
                nc.vector.tensor_reduce(negmax[:], max2[:, j % 2], axis=AX.X, op=ALU.max, negate=True).then_inc(max_ready, 1)

            def invert_sums(pair, r):
                dve.wait_ge(oT_copied, pair + 1)
                ge(dve, o_normed, pair)
                nc.vector.reciprocal(rec[:], OT_s[:, r].rearrange("p (t c) -> p t c", c=VC)[:, :, 2 * DK:2 * DK + 2]
                                     ).then_inc(o_rec, 1)

            def slot(q, j):
                u = q * SLOTS + j
                for i in range(TPB):
                    max_tile(u + 2, i, j)
                    if i == 0:
                        max_end(u + 1, (j + 1) % 2)
                    if i == 6 and j % 2 == 0 and not (isinstance(u, int) and u == 0):
                        invert_sums(q * 2 + j // 2 - 1, (j // 2 + 1) % 2)

            for i in range(TPB):
                max_tile(0, i, 0)
            max_end(0, 0)
            for i in range(TPB):
                max_tile(1, i, 1)
            for j in range(SLOTS):
                slot(0, j)
            with dve.Fori(1, QUADS - 1) as q:
                for j in range(SLOTS):
                    slot(q, j)
            for j in range(SLOTS - 2):
                slot(QUADS - 1, j)
            max_end(NU - 1, 1)
            invert_sums(NPAIR - 2, 0)
            invert_sums(NPAIR - 1, 1)

            base1 = B * LN_STEPS
            dve.wait_ge(bo_ok, B)
            for b in range(B):
                dve.wait_ge(y_ps, b + 1)
                xb = X[:, b * TPB:(b + 1) * TPB].rearrange("p t d -> p (t d)")
                nc.vector.tensor_tensor(xb, xb, ST[b % 2][:], ALU.add).then_inc(x1_ok, 1)
                dve.wait_ge(x1_ok, b + 1)
                norm(lambda t: X[:, b * TPB + t], lambda t: U2[:, b * TPB + t], base1 + 2 * b * LN_STEPS, B + 2 * b)
                nc.vector.tensor_copy(newt[:], rstd[:]).then_inc(u_ok, 1)
                norm(lambda t: U2[:, b * TPB + t], lambda t: XN[:, b * TPB + t],
                     base1 + (2 * b + 1) * LN_STEPS, B + 2 * b + 1)

            step = chain(dve, dve_step, base1 + B * 2 * LN_STEPS)
            dve.wait_ge(aff_ok, B)
            step(nc.vector.tensor_reduce(top[:], aff[:], axis=AX.X, op=ALU.max))
            nc.vector.tensor_tensor(eq[:], aff[:], top[:].unsqueeze(2).to_broadcast([P, T, E]), ALU.is_ge).then_inc(gate_ok, 1)
            dve.wait_ge(gate_ok, 1)
            step(nc.vector.tensor_tensor(eq[:], eq[:], first_w[:].unsqueeze(1).to_broadcast([P, T, E]), ALU.mult))
            step(nc.vector.tensor_reduce(pick[:], eq[:], axis=AX.X, op=ALU.max))
            step(nc.vector.tensor_tensor(hot[:], eq[:], pick[:].unsqueeze(2).to_broadcast([P, T, E]), ALU.is_equal))
            nc.vector.tensor_copy(hotb[:], hot[:]).then_inc(hot_ok, 1)
            dve.wait_ge(rank_ps, 1)
            step(nc.vector.tensor_copy(tot[:], SC[1][:, 0:T * E].rearrange("p (t e) -> p e t", e=E)))
            flat = "p e t -> p (e t)"
            step(nc.vector.tensor_tensor_scan(cum[:].rearrange(flat), tot[:].rearrange(flat), zrow[:], 0.0, ALU.add, ALU.add))
            step(nc.vector.tensor_tensor(cum[:], cum[:], tot[:], ALU.subtract))
            step(nc.vector.tensor_reduce(cnt[:], tot[:], axis=AX.X, op=ALU.add))
            step(nc.vector.tensor_scalar(cnt[:], cnt[:], float(P - 1), None, ALU.add))
            step(nc.vector.tensor_copy(cnti[:], cnt[:]))
            step(nc.vector.tensor_scalar(cnti[:], cnti[:], 7, 7, ALU.logical_shift_right, ALU.logical_shift_left))
            step(nc.vector.tensor_copy(padded[:], cnti[:]))
            step(nc.vector.tensor_tensor_scan(ends[:], padded[:], zrow[:, 0:E], 0.0, ALU.add, ALU.add))
            step(nc.vector.tensor_tensor(start[:], ends[:], padded[:], ALU.subtract))
            step(nc.vector.tensor_tensor(cstart[:], start[:], cum[:, :, 0], ALU.subtract))
            step(nc.vector.tensor_tensor(cum[:], cum[:], cstart[:].unsqueeze(2).to_broadcast([P, E, T]), ALU.add))
            step(nc.vector.tensor_tensor(place[:], SC[0][:, 0:T * E].rearrange("p (t e) -> p t e", e=E),
                                         cum[:].rearrange("p e t -> p t e"), ALU.add))
            step(nc.vector.tensor_tensor(place[:], place[:], hot[:], ALU.mult))
            step(nc.vector.tensor_reduce(slot_f[:], place[:], axis=AX.X, op=ALU.add))
            nc.vector.tensor_copy(slot_i[:], slot_f[:]).then_inc(slots_ok, 1)
            step(nc.vector.tensor_tensor(tile_cmp[:], tile_at[:].unsqueeze(2).to_broadcast([P, SORTED, E]),
                                         start[:].unsqueeze(1).to_broadcast([P, SORTED, E]), ALU.is_ge))
            step(nc.vector.tensor_reduce(tile_ef[:], tile_cmp[:], axis=AX.X, op=ALU.add))
            step(nc.vector.tensor_scalar(tile_ef[:], tile_ef[:], -1.0, None, ALU.add))
            nc.vector.tensor_copy(tile_e[:], tile_ef[:]).then_inc(slots_ok, 1)

            dve.wait_ge(ffn_in, 16 * FFN_LOADS)
            dve.wait_ge(b1_in, 16)
            dve.wait_ge(slots_ok, 2)

            def add_b1(n, i):
                e = dve.value_load(tile_e[0:1, bass.ds(n, 1)], min_val=0, max_val=E - 1)
                dve.wait_ge(h_ps, n + 1)
                ge(dve, ht_ps, n - 1)
                nc.vector.tensor_tensor(hs[:, i], ST[i][:, 0:HALF], b1_s[:, bass.ds(e * F, F)],
                                        ALU.add).then_inc(h_sb, 1)

            def add_b2(n, i, sent):
                e = dve.value_load(tile_e[0:1, bass.ds(n, 1)], min_val=0, max_val=E - 1)
                dve.wait_ge(f_ps, n + 1)
                ge(dve, ys_out[i], sent)
                nc.vector.tensor_tensor(ys[:, i], (OB, MB)[i][:, 0:D], b2_s[:, bass.ds(e * D, D)],
                                        ALU.add).then_inc(f_sb, 1)

            def step(n, i):
                if not isinstance(n, int) or n < SORTED:
                    add_b1(n, i)
                if not isinstance(n, int) or n >= 2:
                    add_b2(n - 2, i, (n // 2 - 1) * 16 if isinstance(n, int) else (n + (-2 - i)) * 8)

            staged(dve, step)

            dve.wait_ge(act_step, 1)
            dve.wait_ge(res_ok, B)
            dve.wait_ge(gathered, 16 * T)
            for b in range(B):
                for t in range(b * TPB, (b + 1) * TPB):
                    last = nc.vector.scalar_tensor_tensor(yg[:, t], yg[:, t], alpha[:, t:t + 1], X[:, t], ALU.mult, ALU.add)
                last.then_inc(final_ok, 1)

        @block.tensor
        def _(pe):
            mm = nc.tensor.matmul
            pe.wait_ge(consts, CONSTS)
            pe.wait_ge(w_in, 16 * W_LOADS)
            for b in range(B):
                pe.wait_ge(normed, b + 1)
                for c in range(2):
                    ge(pe, xnT_sb, 2 * b)
                    for t in range(4):
                        last = nc.tensor.transpose(SC[c][:, t * P:(t + 1) * P], XN[:, b % 2 * TPB + 4 * c + t], ident[:])
                    last.then_inc(xnT_ps, 1)
                pe.wait_ge(xnT_sb, 2 * b + 2)
                for i, w in enumerate((wq_s, wk_s)):
                    ge(pe, full_ok, 2 * b)
                    for c in range(2):
                        last = mm(ST[i][:, c * HALF:(c + 1) * HALF], w[:], xnT[:, c * HALF:(c + 1) * HALF],
                                  start=True, stop=True)
                    last.then_inc(qk_ps, 1)
                for c, bank in enumerate((OB, MB)):
                    ge(pe, v_ok, 2 * b)
                    for t in range(4):
                        last = mm(bank[:, t * P:(t + 1) * P], xnT[:, (4 * c + t) * P:(4 * c + t + 1) * P], wv_s[:],
                                  start=True, stop=True)
                    last.then_inc(v_ps, 1)

            pe.wait_ge(v_ok, 2 * B)
            pe.wait_ge(table_in, 16 * 3)
            for at, src in ((0, cent_s), (64, gb_s)):
                n = src.shape[0]
                nc.tensor.transpose(OB[:, at:at + n], src[:], ident[0:n, 0:n]).then_inc(table_T, 1)
            pe.wait_ge(table_out, TABLES)

            def scores(n, i, j, halves=(0, 1)):
                for c in halves:
                    ge(pe, s_read, n * (2 * TPB) + 2 * i + c - 1)
                    mm(SC[c][:], QA[0:SHIFT, j, i * P:(i + 1) * P], KA[0:SHIFT, j, c * HALF:(c + 1) * HALF],
                       start=True, stop=True).then_inc(s_written, 1)

            def transpose_shift(n):
                pe.wait_ge(mparts_ready, n + 1)
                ge(pe, mT_copied, n)
                nc.tensor.transpose(MT, mparts[:].rearrange("p i t -> p (i t)"), identb[:]).then_inc(mT_written, 1)

            def scores_T(u, i, j):
                ge(pe, p_ready, u * TPB + i - 1)
                for c in range(2):
                    last = mm(ST[i % 2][:, c * HALF:(c + 1) * HALF], KA[:, j, i * P:(i + 1) * P],
                              QA[:, j, c * HALF:(c + 1) * HALF], start=True, stop=True)
                last.then_inc(st_written, 1)

            def weigh(u, i, j):
                pe.wait_ge(p_ready, u * TPB + i + 1)
                if i == 0:
                    pe.wait_ge(v_ready, u + 1)
                for g in range(4):
                    last = mm(OB[g * VC:(g + 1) * VC, 0:QUART], Vst[:, j, i, :],
                              probs[:, i % 2, g * QUART:(g + 1) * QUART],
                              start=(i == 0 and j % 2 == 0), stop=(i == TPB - 1 and j % 2 == 1))
                last.then_inc(pv_done, 1)

            def transpose_o(pair):
                pe.wait_ge(o_copied, pair + 1)
                ge(pe, oT_copied, pair)
                for c in range(2):
                    last = nc.tensor.transpose(MB[:, c * P:(c + 1) * P], O_s[:, c * P:(c + 1) * P], ident[:])
                last.then_inc(o_transposed, 1)

            def slot(q, j, last=False):
                u = q * SLOTS + j
                first = isinstance(u, int) and u == 0
                pe.wait_ge(shift_loaded[j], (q + 1) * (16 * PARTS))
                for i in range(TPB):
                    scores_T(u, i, j)
                    ahead = not (last and j >= 2)
                    if ahead and i == 0:
                        pe.wait_ge(qk_loaded[(j + 2) % SLOTS], (q + (j + 2) // SLOTS + 1) * 32)
                    if ahead:
                        scores(u + 2, i, (j + 2) % SLOTS, halves=(0,))
                    if i == 0 and not first:
                        weigh(u - 1, TPB - 1, (j - 1) % SLOTS)
                    if i == 1 and j % 2 == 0:
                        ge(pe, o_copied, q * 2 + j // 2)
                    if i > 0:
                        weigh(u, i - 1, j)
                    if ahead:
                        scores(u + 2, i, (j + 2) % SLOTS, halves=(1,))
                    if i == SHIFT_AT and not (last and j == SLOTS - 1):
                        transpose_shift(u + 1)
                    if i == SHIFT_AT + 2 and j % 2 == 0 and not first:
                        pe.wait_ge(mT_copied, u + 2)
                        transpose_o(q * 2 + j // 2 - 1)

            pe.wait_ge(qk_loaded[0], 32)
            for i in range(TPB):
                scores(0, i, 0)
            pe.wait_ge(qk_loaded[1], 32)
            for i in range(TPB):
                scores(1, i, 1)
                if i == 3:
                    transpose_shift(0)
            for j in range(SLOTS):
                slot(0, j)
            with pe.Fori(1, QUADS - 1) as q:
                for j in range(SLOTS):
                    slot(q, j)
            for j in range(SLOTS):
                slot(QUADS - 1, j, last=True)
            weigh(NU - 1, TPB - 1, SLOTS - 1)
            transpose_o(NPAIR - 1)

            def project_a(b):
                for c in range(2):
                    ge(pe, a_sb, 2 * b)
                    for t in range(4):
                        qt = 4 * c + t
                        last = nc.tensor.transpose(SC[c][:, t * P:(t + 1) * P], A[:, b * TPB + qt % 2 * 4 + qt // 2], ident[:])
                    last.then_inc(a_ps, 1)
                pe.wait_ge(a_sb, 2 * b + 2)
                ge(pe, x1_ok, b - 1)
                for t in range(TPB):
                    last = mm(ST[b % 2][:, t * P:(t + 1) * P], xnT[:, t * P:(t + 1) * P], wo_s[:], start=True, stop=True)
                last.then_inc(y_ps, 1)

            def affinities(b):
                pe.wait_ge(u_ok, b + 1)
                ge(pe, aff_ok, b)
                for c, bank in enumerate((OB, MB)):
                    for t in range(4):
                        last = nc.tensor.transpose(bank[:, t * P:(t + 1) * P], U2[:, b * TPB + 4 * c + t], ident[:])
                    last.then_inc(u_ps, 1)
                pe.wait_ge(u_sb, 2 * b + 2)
                for t in range(TPB):
                    last = mm(OB[:, t * E:(t + 1) * E], probs[:, 0, t * P:(t + 1) * P], centT[:], start=True, stop=True)
                last.then_inc(aff_ps, 1)

            pe.wait_ge(o_normed, NPAIR)
            project_a(0)
            for b in range(B):
                if b + 1 < B:
                    project_a(b + 1)
                affinities(b)

            pe.wait_ge(hot_ok, 1)
            mm(SC[0][:, 0:T * E], before[:], hotb[:].rearrange("p t e -> p (t e)"), start=True, stop=True)
            mm(SC[1][:, 0:T * E], onesb[:], hotb[:].rearrange("p t e -> p (t e)"), start=True, stop=True).then_inc(rank_ps, 1)
            pe.wait_ge(slots_ok, 1)

            pe.wait_ge(slots_ok, 2)
            pe.wait_ge(ffn_in, 16 * FFN_LOADS)

            def take_x(n, i, loaded):
                pe.wait_ge(xs_in[i], loaded)
                ge(pe, xs_sb, n - 1)
                nc.tensor.transpose(SC[i][:, 0:P], xs[:, i], ident[:]).then_inc(xs_ps, 1)

            def hidden(n, i):
                e = pe.value_load(tile_e[0:1, bass.ds(n, 1)], min_val=0, max_val=E - 1)
                pe.wait_ge(xs_sb, n + 1)
                ge(pe, h_sb, n - 1)
                mm(ST[i][:, 0:HALF], xsT[:, i], w1_s[:, bass.ds(e * F, F)], start=True, stop=True).then_inc(h_ps, 1)

            def transpose_h(n, i):
                pe.wait_ge(h_sb, n + 1)
                ge(pe, ht_sb, n - 1)
                for c in range(FC):
                    last = nc.tensor.transpose(ST[i][:, HALF + c * P:HALF + (c + 1) * P], hs[:, i, c * P:(c + 1) * P], ident[:])
                last.then_inc(ht_ps, 1)

            def project(n, i):
                e = pe.value_load(tile_e[0:1, bass.ds(n, 1)], min_val=0, max_val=E - 1)
                pe.wait_ge(ht_sb, n + 1)
                ge(pe, f_sb, n - 1)
                for c in range(FC):
                    last = mm((OB, MB)[i][:, 0:D], hT[:, i, c * P:(c + 1) * P], w2_s[:, bass.ds(e * F + c * D, D)],
                              start=(c == 0), stop=(c == FC - 1))
                last.then_inc(f_ps, 1)

            def step(n, i):
                known = isinstance(n, int)
                if not known or n + 1 < SORTED:
                    take_x(n + 1, 1 - i, ((n + 1) // 2 + 1) * 16 if known else (n + (3 - (1 - i))) * 8)
                if not known or n < SORTED:
                    hidden(n, i)
                if not known or 0 <= n - 1 < SORTED:
                    transpose_h(n - 1, 1 - i)
                if not known or n >= 2:
                    project(n - 2, i)

            take_x(0, 0, 16)
            staged(pe, step)


_INS = ['L0_attn_x', 'L0_attn_Wq', 'L0_attn_bq', 'L0_attn_Wk', 'L0_attn_bk', 'L0_attn_Wv', 'L0_attn_bv', 'L0_attn_Wo',
        'L0_attn_bo', 'L0_ffn_centroids', 'L0_ffn_ln_g', 'L0_ffn_ln_b', 'L0_ffn_w1', 'L0_ffn_b1', 'L0_ffn_w2', 'L0_ffn_b2']


def kernel(**inputs):
    import numpy as _np
    import concourse.bacc as _bacc
    from concourse import mybir as _mybir
    from concourse.bass_utils import run_bass_kernel_spmd as _run

    nc = _bacc.Bacc("TRN2", target_bir_lowering=False, num_devices=1)
    arrays, args = {}, []
    for name in _INS:
        a = _np.ascontiguousarray(inputs[name])
        arrays[f"in_{name}"] = a
        args.append(nc.dram_tensor(f"in_{name}", a.shape, _mybir.dt.from_np(a.dtype), kind="ExternalInput").ap())
    out = nc.dram_tensor("out_y", inputs["L0_attn_x"].shape, _mybir.dt.float32, kind="ExternalOutput").ap()
    build(nc, *args, out)
    r = _run(nc, [arrays], core_ids=[0])
    return r.results[0]["out_y"]
```

```python
import concourse.bass as bass
import concourse.mybir as mybir
from contextlib import ExitStack

F32 = mybir.dt.float32
BF16 = mybir.dt.bfloat16
I32 = mybir.dt.int32
ALU = mybir.AluOpType
ACT = mybir.ActivationFunctionType
AX = mybir.AxisListType

P = 128
B, S, D = 4, 1024, 128
H = 16
DK = D // H
E, F = 8, 512
EPS = 1e-5
TPB = S // P
T = B * TPB
NU = B * H
NPAIR = NU // 2
PARTS = 3
ROWS = PARTS * PARTS * DK
SHIFT = 96
SLOTS = 4
QUADS = NU // SLOTS
VC = 32
QUART = S // 4
HALF = 512
FC = F // P
SORTED = T + E - 1
RING = 8
FULL = (SORTED - 5 - RING) // RING * RING
ROW = 2 * D + 1
SHIFT_AT = 2
SCALE = float(DK) ** -0.5


def ge(eng, sem, value):
    if isinstance(value, int) and value <= 0:
        return
    eng.wait_ge(sem, value)


def bare(eng, held, *waits):
    waits = [(s, v) for s, v in waits if not (isinstance(v, int) and v <= 0)]
    waits = [(s, v if isinstance(v, int) else eng.to_reg(v)) for s, v in waits]
    eng.wait_ge(*held)
    for s, v in waits:
        eng.wait_ge(s, v)


def staged(eng, step):
    for n in range(RING):
        step(n, 0, n)
    with eng.Fori(1, FULL // RING + 1) as q:
        for j in range(RING):
            step(q * RING + j, q, j)
    for n in range(RING + FULL, SORTED + 2):
        step(n, n // RING, n % RING)


def chain(eng, sem, base=0):
    n = [0]

    def step(ins):
        n[0] += 1
        ins.then_inc(sem, 1)
        eng.wait_ge(sem, base + n[0])
    step.count = n
    return step


def build(nc, x, Wq, bq, Wk, bk, Wv, bv, Wo, bo, cent, ln_g, ln_b, w1, b1, w2, b2, out):
    ctx = ExitStack()
    with ctx:
        def sb(name, shape, dt=F32):
            return ctx.enter_context(nc.sbuf_tensor(name, shape, dt))

        def sem(name):
            return ctx.enter_context(nc.semaphore(name))

        q_parts = nc.dram_tensor("q_parts", (NU, PARTS, DK, S), BF16, kind="Internal").ap()
        k_parts = nc.dram_tensor("k_parts", (NU, DK, PARTS, S), BF16, kind="Internal").ap()
        token_rows = nc.dram_tensor("token_rows", (T * P, ROW), F32, kind="Internal").ap()

        wq_s, wk_s, wv_s, wo_s = (sb(n, [P, D]) for n in ("wq_s", "wk_s", "wv_s", "wo_s"))
        bq_s, bk_s = sb("bq_s", [P, 1]), sb("bk_s", [P, 1])
        bv_s, bo_s = sb("bv_s", [P, D]), sb("bo_s", [P, D])
        cent_s, centT = sb("cent_s", [E, D]), sb("centT", [P, E])
        gb_s, gbT = sb("gb_s", [2 * E, D]), sb("gbT", [P, 2 * E])
        b2_s = sb("b2_s", [P, E * D])
        w1_s, w2_s = sb("w1_s", [P, E * F]), sb("w2_s", [P, E * F])
        ident, identb = sb("ident", [P, P]), sb("identb", [P, P], BF16)
        before = sb("before", [P, P], BF16)
        onesb = sb("onesb", [P, P], BF16)
        prow, page = sb("prow", [P, P], BF16), sb("page", [P, SORTED], BF16)
        idle = sb("idle", [P, 2])
        tile1, pcol = sb("tile1", [P, T], BF16), sb("pcol", [P, 1])

        X = sb("X", [P, T, D])
        sent = sb("sent", [P, T, ROW])
        early = sent[:].rearrange("p t c -> p (t c)")
        Vall = early[:, 0:NU * TPB * DK]
        x_normed = early[:, NU * TPB * DK:NU * TPB * DK + 2 * TPB * D].rearrange("p (t d) -> p t d", d=D)
        A = sb("A", [P, T, D])
        U2 = sb("U2", [P, T, D])
        stats, mv = sb("stats", [P, TPB, 6]), sb("mv", [P, TPB, 2])
        rstd, vpe, root, newt = (sb(n, [P, TPB]) for n in ("rstd", "vpe", "root", "newt"))
        xnT = sb("xnT", [P, S])
        work = sb("work", [P, 4, S])
        full = [work[:, 0:2], A[:, 0:TPB * 2].rearrange("p t c -> p (t c)").rearrange("p (i s) -> p i s", i=2)]
        rest = [work[:, 2:4], A[:, TPB * 2:T].rearrange("p t c -> p (t c)").rearrange("p (i s) -> p i s", i=2)]
        parts = [sb("parts", [P, 2, PARTS, S], BF16)[:],
                 U2[:].rearrange("p t c -> p (t c)").bitcast(BF16)[:, 0:2 * PARTS * S]
                 .rearrange("p (i j s) -> p i j s", i=2, j=PARTS)]
        norms_at = parts[0].rearrange("p i j s -> p (i j s)").bitcast(F32)
        mv2 = norms_at[:, 0:4 * T].rearrange("p (k t c) -> p k t c", k=2, c=2)
        vpe2, root2, scale2, newt2, shift2 = (
            norms_at[:, (4 + 2 * i) * T:(6 + 2 * i) * T].rearrange("p (k t) -> p k t", k=2) for i in range(5))
        b1_s = work[:].rearrange("p i s -> p (i s)")
        QA, KA = sb("QA", [P, SLOTS, S], BF16), sb("KA", [P, SLOTS, S], BF16)
        Vst = sb("Vst", [P, SLOTS, TPB, VC])
        probs = sb("probs", [P, 2, S])
        max2 = sb("max2", [P, 2, TPB, 2])
        negmax, mrest = sb("negmax", [P, TPB]), sb("mrest", [P, 2, TPB])
        mparts = sb("mparts", [P, PARTS, TPB], BF16)
        shiftT = sb("shiftT", [PARTS * TPB, SLOTS, P], BF16)
        O_s = sb("O_s", [P, QUART])
        rec = sb("rec", [P, TPB, 2])
        OT_s = sb("OT_s", [P, 2, QUART])

        aff, eq = sb("aff", [P, T, E]), sb("eq", [P, T, E])
        pick = sb("pick", [P, T])
        first_w = sb("first_w", [P, E])
        hot, hotb = sb("hot", [P, T, E]), sb("hotb", [P, T, E], BF16)
        tot, cum = sb("tot", [P, E, T]), sb("cum", [P, E, T])
        zrow = sb("zrow", [P, E * T])
        cnt, cnti = sb("cnt", [P, E]), sb("cnti", [P, E], I32)
        padded, ends, start = sb("padded", [P, E]), sb("ends", [P, E]), sb("start", [P, E])
        cstart = sb("cstart", [P, E])
        place, slot_f, slot_i = sb("place", [P, T, E]), sb("slot_f", [P, T]), sb("slot_i", [P, T], I32)
        slot_page, slot_at = sb("slot_page", [P, T], BF16), sb("slot_at", [P, T], BF16)
        at_one = probs[:].rearrange("p i s -> p (i s)").bitcast(BF16).rearrange("p (t s) -> p t s", s=P)
        page_one = QA[:].rearrange("p j s -> p (j s)")[:, 0:T * SORTED].rearrange("p (t n) -> p t n", n=SORTED)
        page_id = KA[:].rearrange("p j s -> p (j s)")[:, 0:T * 2 * SORTED].rearrange("p (t i n) -> p t i n", i=2, n=SORTED)
        token_f, vacant = sb("token_f", [P, SORTED]), sb("vacant", [P, SORTED])
        token = sb("token", [P, SORTED], I32)
        tile_at, tile_cmp = sb("tile_at", [P, SORTED]), sb("tile_cmp", [P, SORTED, E])
        tile_ef, tile_e = sb("tile_ef", [P, SORTED]), sb("tile_e", [P, SORTED], I32)

        xs, gate = sb("xs", [P, RING, ROW]), sb("gate", [P, RING])
        token_from, token_to = sb("token_from", [P, RING], I32), sb("token_to", [P, RING], I32)
        xsT = sb("xsT", [P, 2, P])
        hs = A[:, 0:TPB].rearrange("p (i c) d -> p i (c d)", i=2)
        hT = A[:, TPB:2 * TPB].rearrange("p (i c) d -> p i (c d)", i=2)
        yb, ys = sb("yb", [P, D]), A[:, 2 * TPB:2 * TPB + RING]

        ST = [ctx.enter_context(nc.psum_tensor(f"ST{i}", [P, S], F32)) for i in range(2)]
        SC = [ctx.enter_context(nc.psum_tensor(f"SC{i}", [P, HALF], F32)) for i in range(2)]
        OB = ctx.enter_context(nc.psum_tensor("OB", [P, HALF], F32))
        MB = ctx.enter_context(nc.psum_tensor("MB", [P, HALF], F32))
        MT = MB[0:PARTS * TPB, 2 * P:2 * P + P // 2].bitcast(BF16)

        x_in = [sem(f"x_in{b}") for b in range(B)]
        w_in, ffn_in, b1_in = sem("w_in"), sem("ffn_in"), sem("b1_in")
        rows_set = sem("rows_set")
        consts, table_in, table_T, table_out = sem("consts"), sem("table_in"), sem("table_T"), sem("table_out")
        pool_step, dve_step = sem("pool_step"), sem("dve_step")
        var_ok, root_ok = sem("var_ok"), sem("root_ok")
        normed, xnT_ps, xnT_sb = sem("normed"), sem("xnT_ps"), sem("xnT_sb")
        qk_ps, v_ps, full_ok, v_ok = sem("qk_ps"), sem("v_ps"), sem("full_ok"), sem("v_ok")
        part1, rest_q, rest_k, part2, part3 = (sem(n) for n in ("part1", "rest_q", "rest_k", "part2", "part3"))
        first_out = sem("first_out")
        parts_out = [sem(f"parts_out{b}") for b in range(B)]
        bo_ok = sem("bo_ok")
        qk_loaded = [sem(f"qk_loaded{j}") for j in range(SLOTS)]
        shift_loaded = [sem(f"shift_loaded{j}") for j in range(SLOTS)]
        s_written, s_read = sem("s_written"), sem("s_read")
        st_written, p_ready, pv_done = sem("st_written"), sem("p_ready"), sem("pv_done")
        v_ready, max_ready, mparts_ready = sem("v_ready"), sem("max_ready"), sem("mparts_ready")
        mT_written, mT_copied = sem("mT_written"), sem("mT_copied")
        o_copied, o_transposed, oT_copied = (sem(n) for n in ("o_copied", "o_transposed", "oT_copied"))
        o_rec, o_normed = sem("o_rec"), sem("o_normed")
        a_ps, a_sb, y_ps, x1_ok = sem("a_ps"), sem("a_sb"), sem("y_ps"), sem("x1_ok")
        u_ok, u_ps, u_sb, aff_ps, aff_ok, xn_ok = (sem(n) for n in ("u_ok", "u_ps", "u_sb", "aff_ps", "aff_ok", "xn_ok"))
        res_ok, hot_ok, rank_ps, slots_ok = (sem(n) for n in ("res_ok", "hot_ok", "rank_ps", "slots_ok"))
        ones_ok, token_ps, token_ok, rows_out = (sem(n) for n in ("ones_ok", "token_ps", "token_ok", "rows_out"))
        xs_in = [sem(f"xs_in{i}") for i in range(RING)]
        ys_out = [sem(f"ys_out{i}") for i in range(RING)]
        u2_ok = sem("u2_ok")
        yb_ok, coef_ok, top_ok = sem("yb_ok"), sem("coef_ok"), sem("top_ok")
        from_ok, to_ok = sem("from_ok"), sem("to_ok")
        xs_ps, xs_sb, h_ps, h_sb, ht_ps, ht_sb, f_ps, f_sb = (
            sem(n) for n in ("xs_ps", "xs_sb", "h_ps", "h_sb", "ht_ps", "ht_sb", "f_ps", "f_sb"))

        W_LOADS, FFN_LOADS, CONSTS = 8, 3, 12
        TABLES = 2
        U, XN = 0, 1
        NORMS = [(U, 0, (B - 1) * TPB), (U, (B - 1) * TPB, T)] + [(XN, b * TPB, (b + 1) * TPB) for b in range(B)]

        def wait_u(eng, b):
            eng.wait_ge(*((u_ok, 1), (u_ok, 2), (u2_ok, 1), (u_ok, 3))[b])

        block = ctx.enter_context(nc.Block())

        @block.sync
        def _(sp):
            def load_tokens(b):
                sp.dma_start(X[:, b * TPB:(b + 1) * TPB], x[b].rearrange("(t p) d -> p t d", p=P)).then_inc(x_in[b], 16)

            load_tokens(0)
            for dst, src in ((wq_s, Wq), (wk_s, Wk)):
                sp.dma_start(dst[:], src).then_inc(w_in, 16)
            for dst, src in ((bq_s, bq), (bk_s, bk)):
                sp.dma_start(dst[:], src.rearrange("(p a) -> p a", a=1)).then_inc(w_in, 16)
            load_tokens(1)
            for dst, src in ((wv_s, Wv), (wo_s, Wo)):
                sp.dma_start(dst[:], src).then_inc(w_in, 16)
            for dst, src in ((bv_s, bv), (bo_s, bo)):
                sp.dma_start(dst[:], src.partition_broadcast(P)).then_inc(w_in, 16)
            load_tokens(2)
            load_tokens(3)
            sp.dma_start(cent_s[:], cent).then_inc(table_in, 16)
            sp.dma_start(gb_s[0:E, :], ln_g).then_inc(table_in, 16)
            sp.dma_start(gb_s[E:2 * E, :], ln_b).then_inc(table_in, 16)

            sp.dma_start(w1_s[:].rearrange("p (e f) -> p e f", e=E), w1.rearrange("e p f -> p e f")).then_inc(ffn_in, 16)
            sp.dma_start(w2_s[:].rearrange("p (e c d) -> p e c d", e=E, c=FC),
                         w2.rearrange("e (c p) d -> p e c d", p=P)).then_inc(ffn_in, 16)
            sp.dma_start(b2_s[:], b2.rearrange("e d -> (e d)").partition_broadcast(P)).then_inc(ffn_in, 16)

            def store_parts(b, first=0, last=H, done=None):
                rows = slice(first * DK, last * DK)
                units = slice(b * H + first, b * H + last)
                done = done or parts_out[b]
                for i in range(PARTS):
                    sp.dma_start(q_parts[units, i], parts[b % 2][rows, 0, i]).then_inc(done, 16)
                sp.dma_start(k_parts[units].rearrange("h d j s -> (h d) (j s)"),
                             parts[b % 2][rows, 1].rearrange("p j s -> p (j s)")).then_inc(done, 16)

            def load(n, j):
                ge(sp, st_written, TPB * (n - SLOTS + 1))
                sp.dma_start(QA[0:ROWS, j],
                             q_parts[bass.ds(n, 1)].rearrange("a i d s -> (a i d) s").unsqueeze(1)
                             .to_broadcast([PARTS * DK, PARTS, S])).then_inc(qk_loaded[j], 16)
                sp.dma_start(KA[0:ROWS, j],
                             k_parts[bass.ds(n, 1)].rearrange("a d j s -> a (d j) s")
                             .to_broadcast([PARTS, DK * PARTS, S])).then_inc(qk_loaded[j], 16)

            def shift(n, j):
                sp.wait_ge(mT_copied, n + 1)
                for i in range(PARTS):
                    sp.dma_start(QA[SHIFT + i:SHIFT + i + 1, j, :].rearrange("a (t q) -> a t q", t=TPB),
                                 shiftT[TPB * i:TPB * (i + 1), j, :]).then_inc(shift_loaded[j], 16)

            sp.wait_ge(part3, 2)
            store_parts(0, last=SLOTS, done=first_out)
            sp.wait_ge(rows_set, 2)
            sp.wait_ge(first_out, 16 * (PARTS + 1))
            for n in range(2):
                load(n, n)
            store_parts(0, first=SLOTS)
            for n in range(2, SLOTS):
                load(n, n)
            for b in range(1, B - 1):
                sp.wait_ge(part3, 2 * b + 2)
                store_parts(b)
            shift(0, 0)
            sp.wait_ge(part3, 2 * B)
            store_parts(B - 1)
            for b in range(B - 1):
                sp.wait_ge(parts_out[b], 16 * (PARTS + 1))

            def slot(u, j, last=False):
                if not (last and j > 0) and not (isinstance(u, int) and u == 0):
                    load(u + 3, (j + 3) % SLOTS)
                if not (last and j == SLOTS - 1):
                    shift(u + 1, (j + 1) % SLOTS)

            for j in range(SLOTS):
                slot(j, j)
            sp.wait_ge(parts_out[B - 1], 16 * (PARTS + 1))
            sp.dma_start(b1_s, b1.rearrange("e f -> (e f)").partition_broadcast(P)).then_inc(b1_in, 16)
            with sp.Fori(1, QUADS - 1) as q:
                for j in range(SLOTS):
                    slot(q * SLOTS + j, j)
            for j in range(SLOTS):
                slot(NU - SLOTS + j, j, last=True)

            rows = token_rows.rearrange("(t p) c -> p t c", p=P)
            for b in range(B):
                sp.wait_ge(xn_ok, b + 1)
                sp.wait_ge(res_ok, b + 1)
                sp.wait_ge(top_ok, b + 1)
                sp.dma_start(rows[:, b * TPB:(b + 1) * TPB], sent[:, b * TPB:(b + 1) * TPB]).then_inc(rows_out, 16)
            for j in range(RING):
                sp.wait_ge(ys_out[j], 16 * ((SORTED + RING - 1 - j) // RING))

        @block.gpsimd
        def _(pool):
            nc.gpsimd.memset(ident[:], 0.0).then_inc(pool_step, 1)
            nc.gpsimd.memset(identb[:], 0.0).then_inc(pool_step, 1)
            nc.gpsimd.memset(before[:], 1.0).then_inc(pool_step, 1)
            nc.gpsimd.memset(Vst[:], 0.0).then_inc(pool_step, 1)
            for m, pattern, first, step in ((prow, [[1, P]], 0, 0), (page, [[1, SORTED]], 0, 0),
                                            (tile1, [[1, T]], 1, 0), (pcol, [[0, 1]], 0, 1)):
                nc.gpsimd.iota(m[:], pattern, base=first, channel_multiplier=step,
                               allow_small_or_imprecise_dtypes=True).then_inc(consts, 1)
            nc.gpsimd.memset(onesb[:], 1.0).then_inc(consts, 1)
            nc.gpsimd.memset(zrow[:], 0.0).then_inc(consts, 1)
            nc.gpsimd.iota(first_w[:], [[-1, E]], base=E, channel_multiplier=0,
                           allow_small_or_imprecise_dtypes=True).then_inc(consts, 1)
            nc.gpsimd.iota(tile_at[:], [[P, SORTED]], base=0, channel_multiplier=0,
                           allow_small_or_imprecise_dtypes=True).then_inc(consts, 1)
            pool.wait_ge(pool_step, 4)
            for m in (ident, identb):
                nc.gpsimd.affine_select(out=m[:], in_=m[:], compare_op=ALU.not_equal, fill=1.0, base=0,
                                        pattern=[[-1, P]], channel_multiplier=1).then_inc(consts, 1)
            nc.gpsimd.affine_select(out=before[:], in_=before[:], compare_op=ALU.is_gt, fill=0.0, base=0,
                                    pattern=[[1, P]], channel_multiplier=-1).then_inc(consts, 1)
            for j in range(SLOTS):
                last = nc.gpsimd.memset(Vst[:, j, :, 2 * DK + j % 2:2 * DK + j % 2 + 1], 1.0)
                last.then_inc(consts if j == SLOTS - 1 else pool_step, 1)
            nc.gpsimd.memset(KA[:], 1.0).then_inc(rows_set, 1)
            nc.gpsimd.memset(QA[:], 0.0).then_inc(rows_set, 1)
            nc.gpsimd.memset(xs[:], 0.0).then_inc(pool_step, 1)

            def third_parts(b):
                ring = b % 2
                pool.wait_ge(part1, 2 * b + 2)
                nc.gpsimd.tensor_tensor(rest[ring][:, 1], full[ring][:, 1], parts[ring][:, 1, 0],
                                        ALU.subtract).then_inc(rest_k, 1)
                for i in range(2):
                    pool.wait_ge(part2, 2 * b + i + 1)
                    nc.gpsimd.tensor_tensor(parts[ring][:, i, 2], rest[ring][:, i], parts[ring][:, i, 1],
                                            ALU.subtract).then_inc(part3, 1)

            for b in range(B - 1):
                third_parts(b)

            pool.wait_ge(v_ok, 2 * B)

            MSTEPS = 3

            def norm_o(pair, r):
                pool.wait_ge(o_rec, pair + 1)
                v = OT_s[:, r].rearrange("p (t c) -> p t c", c=VC)
                cols = A[:].rearrange("p (b t) c -> p b t c", b=B)[
                    :, bass.ds(pair // (H // 2), 1), :, bass.ds(pair % (H // 2) * (2 * DK), 2 * DK)]
                nc.gpsimd.tensor_tensor(
                    cols.rearrange("p a t (h d) -> p (a t) h d", h=2),
                    v[:, :, 0:2 * DK].rearrange("p t (h d) -> p t h d", h=2),
                    rec[:].unsqueeze(3).to_broadcast([P, TPB, 2, DK]), ALU.mult).then_inc(o_normed, 1)

            def unit(n, j, pair=None):
                bare(pool, (v_ok, 2 * B), (pv_done, TPB * (n - SLOTS + 1)))
                nc.gpsimd.tensor_copy(Vst[:, j, :, (j % 2) * DK:(j % 2 + 1) * DK],
                                      Vall[:, bass.ds(n * (TPB * DK), TPB * DK)].rearrange("p (t d) -> p t d", d=DK)
                                      ).then_inc(v_ready, 1)
                if j % 2 == 0 and pair is not None:
                    norm_o(pair, j // 2)
                bare(pool, (v_ok, 2 * B), (max_ready, n + 1), (mT_written, n))
                step = chain(pool, pool_step, POOL0 + n * MSTEPS)
                step(nc.gpsimd.tensor_copy(mparts[:, 0], negmax[:]))
                nc.gpsimd.tensor_tensor(mrest[:, 0], negmax[:], mparts[:, 0], ALU.subtract).then_inc(pool_step, 1)
                step.count[0] += 1
                bare(pool, (v_ok, 2 * B), (pool_step, POOL0 + n * MSTEPS + step.count[0]))
                step(nc.gpsimd.tensor_copy(mparts[:, 1], mrest[:, 0]))
                nc.gpsimd.tensor_tensor(mparts[:, 2], mrest[:, 0], mparts[:, 1], ALU.subtract).then_inc(mparts_ready, 1)
                assert step.count[0] == MSTEPS

            POOL0 = 5 + SLOTS - 1
            for j in range(SLOTS):
                unit(j, j)
                if j == 0:
                    third_parts(B - 1)
                    pool.wait_ge(part3, 2 * B)
                nc.gpsimd.tensor_tensor(X[:, j * TPB:(j + 1) * TPB], X[:, j * TPB:(j + 1) * TPB],
                                        bo_s[:].unsqueeze(1).to_broadcast([P, TPB, D]), ALU.add).then_inc(bo_ok, 1)
            assert SLOTS == B
            with pool.Fori(1, QUADS) as q:
                for j in range(SLOTS):
                    unit(q * SLOTS + j, j, pair=q * 2 + (j // 2 - 2))
            norm_o(NPAIR - 2, 0)
            norm_o(NPAIR - 1, 1)

            pool.wait_ge(v_ready, NU)
            assert B == 4
            tiles = slice(2 * TPB, 3 * TPB)
            pool.wait_ge(coef_ok, 1)
            nc.gpsimd.tensor_tensor(U2[:, tiles], X[:, tiles], scale2[:, U, tiles].unsqueeze(2).to_broadcast([P, TPB, D]),
                                    ALU.mult).then_inc(pool_step, 1)
            pool.wait_ge(pool_step, POOL0 + NU * MSTEPS + 1)
            nc.gpsimd.tensor_tensor(U2[:, tiles], U2[:, tiles], shift2[:, U, tiles].unsqueeze(2).to_broadcast([P, TPB, D]),
                                    ALU.add).then_inc(u2_ok, 1)
            for b in range(B):
                wait_u(pool, b)
                tiles = slice(b * TPB, (b + 1) * TPB)
                nc.gpsimd.tensor_tensor(sent[:, tiles, D:2 * D], X[:, tiles], U2[:, tiles], ALU.add).then_inc(res_ok, 1)

            out_rows = out.rearrange("b s d -> (b s) d")

            def gather(n, j):
                bare(pool, (token_ok, 1), (from_ok, n + 1), (f_sb, n + (1 - RING)))
                pool.indirect_dma_start(xs[:, j], None, token_rows, bass.IndirectOffsetOnAxis(token_from[:, j:j + 1], 0),
                                        bounds_check=T * P - 1, oob_is_err=False).then_inc(xs_in[j], 16)

            def scatter(n, j):
                bare(pool, (token_ok, 1), (to_ok, n + 1), (f_sb, n + 1))
                pool.indirect_dma_start(out_rows, bass.IndirectOffsetOnAxis(token_to[:, j:j + 1], 0), ys[:, j], None,
                                        bounds_check=T * P - 1, oob_is_err=False).then_inc(ys_out[j], 16)

            def step(n, q, j):
                if not isinstance(n, int) or n + 4 < SORTED:
                    gather(n + 4, (j + 4) % RING)
                if not isinstance(n, int) or n >= 2:
                    scatter(n - 2, (j - 2) % RING)

            pool.wait_ge(token_ok, 1)
            pool.wait_ge(rows_out, 16 * B)
            for n in range(4):
                gather(n, n)
            staged(pool, step)

        @block.scalar
        def _(act):
            act.wait_ge(consts, 4)
            nc.scalar.activation(idle[:, 0:1], pcol[:], ACT.Sqrt)
            act.wait_ge(w_in, 16 * W_LOADS)
            def take_root(n):
                act.wait_ge(var_ok, n + 1)
                nc.scalar.activation(root[:], vpe[:], ACT.Sqrt).then_inc(root_ok, 1)

            def take_xnT(b):
                for c in range(2):
                    act.wait_ge(xnT_ps, 2 * b + c + 1)
                    nc.scalar.activation(xnT[:, c * HALF:(c + 1) * HALF], SC[c][:], ACT.Copy).then_inc(xnT_sb, 1)

            def take_full(b):
                for i, bias in enumerate((bq_s, bk_s)):
                    act.wait_ge(qk_ps, 2 * b + i + 1)
                    if b >= 2:
                        act.wait_ge(part3, 2 * (b - 1))
                    nc.scalar.activation(full[b % 2][:, i], ST[i][:], ACT.Identity, bias=bias[:]).then_inc(full_ok, 1)

            def take_part1(b):
                if b >= 2:
                    act.wait_ge(parts_out[b - 2], 16 * (PARTS + 1))
                if b == 2:
                    act.wait_ge(first_out, 16 * (PARTS + 1))
                for i in range(2):
                    act.wait_ge(full_ok, 2 * b + i + 1)
                    nc.scalar.activation(parts[b % 2][:, i, 0], full[b % 2][:, i], ACT.Copy).then_inc(part1, 1)

            def take_part2(b):
                for i in range(2):
                    act.wait_ge((rest_q, rest_k)[i], b + 1)
                    nc.scalar.activation(parts[b % 2][:, i, 1], rest[b % 2][:, i], ACT.Copy).then_inc(part2, 1)

            take_root(0)
            take_root(1)
            take_xnT(0)
            take_root(2)
            for b in range(B):
                take_full(b)
                if b + 1 < B:
                    take_xnT(b + 1)
                take_part1(b)
                if b + 3 < B:
                    take_root(b + 3)
                take_part2(b)

            def exp_tile(u, i):
                act.wait_ge(st_written, u * TPB + i + 1)
                ge(act, pv_done, u * TPB + i - 1)
                nc.scalar.activation(probs[:, i % 2], ST[i % 2][:], ACT.Exp, scale=SCALE).then_inc(p_ready, 1)

            def take_o(pair):
                act.wait_ge(pv_done, (pair + 1) * (2 * TPB))
                ge(act, o_transposed, pair)
                nc.scalar.activation(O_s[:], OB[:, 0:QUART], ACT.Copy).then_inc(o_copied, 1)

            def take_shift(n, q, j):
                act.wait_ge(mT_written, n + 1)
                ge(act, shift_loaded[j], q * (16 * PARTS))
                nc.scalar.activation(shiftT[:, j], MT, ACT.Copy).then_inc(mT_copied, 1)

            def take_oT(pair, r):
                act.wait_ge(o_transposed, pair + 1)
                ge(act, o_normed, pair - 1)
                nc.scalar.activation(OT_s[:, r], MB[:, 0:QUART], ACT.Copy).then_inc(oT_copied, 1)

            def slot(q, j, last=False):
                u = q * SLOTS + j
                pair = q * 2 + j // 2 - 1
                for i in range(TPB):
                    exp_tile(u, i)
                    if i == 0 and j % 2 == 0 and not (isinstance(u, int) and u == 0):
                        take_o(pair)
                    if i == SHIFT_AT + 1 and not (last and j == SLOTS - 1):
                        take_shift(u + 1, q + (j + 1) // SLOTS, (j + 1) % SLOTS)
                    if i == SHIFT_AT + 3 and j % 2 == 0 and not (isinstance(u, int) and u == 0):
                        take_oT(pair, (j // 2 + 1) % 2)

            take_shift(0, 0, 0)
            for j in range(SLOTS):
                slot(0, j)
            with act.Fori(1, QUADS - 1) as q:
                for j in range(SLOTS):
                    slot(q, j)
            for j in range(SLOTS):
                slot(QUADS - 1, j, last=True)

            def take_root2(k):
                kind, first, last = NORMS[k]
                act.wait_ge(var_ok, B + k + 1)
                nc.scalar.activation(root2[:, kind, first:last], vpe2[:, kind, first:last], ACT.Sqrt).then_inc(root_ok, 1)

            def apply_norm(src, dst, kind, b, k, done):
                act.wait_ge(coef_ok, k + 1)
                for t in range(b * TPB, (b + 1) * TPB):
                    last = nc.scalar.activation(dst(t), src[:, t], ACT.Identity, bias=shift2[:, kind, t:t + 1],
                                                scale=scale2[:, kind, t:t + 1])
                last.then_inc(done, 1)

            take_root2(0)
            take_o(NPAIR - 1)
            take_oT(NPAIR - 1, 1)
            def take_uT(b):
                act.wait_ge(u_ps, 2 * b + 2)
                ge(act, aff_ps, b - 1)
                nc.scalar.activation(probs[:, b % 2, HALF:S], MB[:], ACT.Copy).then_inc(u_sb, 1)

            for b in range(2):
                apply_norm(X, lambda t: U2[:, t], U, b, 0, u_ok)
            take_uT(0)
            take_root2(1)
            take_uT(1)
            apply_norm(X, lambda t: U2[:, t], U, B - 1, 1, u_ok)
            take_uT(2)
            act.wait_ge(v_ready, NU)
            act.wait_ge(u_ok, B - 1)
            for b in range(B):
                take_root2(2 + b)
                wait_u(act, b)
                apply_norm(U2, lambda t: sent[:, t, 0:D], XN, b, 2 + b, xn_ok)
                if b == 0:
                    take_uT(B - 1)
            nc.scalar.activation(idle[:, 1:2], pcol[:], ACT.Sigmoid)

            act.wait_ge(table_out, TABLES)
            act.wait_ge(slots_ok, 1)

            def gain(n, i, j):
                e = act.value_load(tile_e[0:1, bass.ds(n, 1)], min_val=0, max_val=E - 1)
                act.wait_ge(xs_ps, n + 1)
                nc.scalar.activation(gate[:, j:j + 1], xs[:, j, 2 * D:ROW], ACT.Sigmoid)
                nc.scalar.activation(xsT[:, i], SC[i][:, 0:P], ACT.Identity, bias=gbT[:, bass.ds(e + E, 1)],
                                     scale=gbT[:, bass.ds(e, 1)]).then_inc(xs_sb, 1)

            def relu(n, i):
                act.wait_ge(ht_ps, n + 1)
                nc.scalar.activation(hT[:, i], ST[i][:, HALF:S], ACT.Relu).then_inc(ht_sb, 1)

            def step(n, q, j):
                i = j % 2
                if not isinstance(n, int) or n + 1 < SORTED:
                    gain(n + 1, 1 - i, (j + 1) % RING)
                if not isinstance(n, int) or 0 <= n - 1 < SORTED:
                    relu(n - 1, 1 - i)

            gain(0, 0, 0)
            staged(act, step)

        @block.vector
        def _(dve):
            LN_STEPS = 8

            def norm(src, dst, base, nth):
                step = chain(dve, dve_step, base)
                for t in range(TPB):
                    last = nc.vector.bn_stats(stats[:, t], src(t))
                last.then_inc(dve_step, 1)
                step.count[0] += 1
                dve.wait_ge(dve_step, base + step.count[0])
                for t in range(TPB):
                    last = nc.vector.bn_aggr(mv[:, t], stats[:, t])
                step(last)
                nc.vector.tensor_scalar(vpe[:], mv[:, :, 1], EPS, None, ALU.add).then_inc(var_ok, 1)
                dve.wait_ge(root_ok, nth + 1)
                step(nc.vector.reciprocal(rstd[:], root[:]))
                step(nc.vector.tensor_tensor(newt[:], rstd[:], rstd[:], ALU.mult))
                step(nc.vector.tensor_tensor(newt[:], newt[:], vpe[:], ALU.mult))
                step(nc.vector.tensor_scalar(newt[:], newt[:], -0.5, 1.5, ALU.mult, ALU.add))
                step(nc.vector.tensor_tensor(rstd[:], rstd[:], newt[:], ALU.mult))
                for t in range(TPB):
                    last = nc.vector.tensor_scalar(dst(t), src(t), mv[:, t, 0:1], rstd[:, t:t + 1], ALU.subtract, ALU.mult)
                step(last)
                assert step.count[0] == LN_STEPS

            def tile_of(tensor, b, t):
                return tensor[:, bass.ds(b * TPB + t, 1)].rearrange("p a d -> p (a d)")

            def norm_x(b):
                dve.wait_ge(x_in[b], 16)
                ge(dve, xnT_ps, 2 * (b - 1))
                r = b % 2 * TPB
                norm(lambda t: X[:, b * TPB + t], lambda t: x_normed[:, r + t], b * LN_STEPS, b)
                nc.vector.tensor_copy(newt[:], rstd[:]).then_inc(normed, 1)

            def take_values(b, banks=(0, 1)):
                for c in banks:
                    dve.wait_ge(v_ps, 2 * b + c + 1)
                    nc.vector.tensor_tensor(
                        Vall[:, b * (H * TPB * DK):(b + 1) * (H * TPB * DK)]
                        .rearrange("p (h t d) -> p h t d", h=H, t=TPB)[:, :, 4 * c:4 * c + 4, :]
                        .rearrange("p h t d -> p t h d"),
                        (OB, MB)[c][:].rearrange("p (t h d) -> p t h d", t=4, h=H),
                        bv_s[:].rearrange("p (h d) -> p h d", h=H).unsqueeze(1).to_broadcast([P, 4, H, DK]),
                        ALU.add).then_inc(v_ok, 1)

            def take_rest(b):
                dve.wait_ge(part1, 2 * b + 1)
                nc.vector.tensor_tensor(rest[b % 2][:, 0], full[b % 2][:, 0], parts[b % 2][:, 0, 0],
                                        ALU.subtract).then_inc(rest_q, 1)

            def max_tile(n, i, j):
                for c in range(2):
                    dve.wait_ge(s_written, n * (2 * TPB) + 2 * i + c + 1)
                    nc.vector.tensor_reduce(max2[:, j % 2, i, c:c + 1], SC[c][:], axis=AX.X, op=ALU.max).then_inc(s_read, 1)

            def max_end(n, j):
                dve.wait_ge(s_read, (n + 1) * (2 * TPB))
                ge(dve, mparts_ready, n)
                nc.vector.tensor_reduce(negmax[:], max2[:, j % 2], axis=AX.X, op=ALU.max, negate=True).then_inc(max_ready, 1)

            norm_x(0)
            norm_x(1)
            norm_x(2)
            dve.wait_ge(w_in, 16 * W_LOADS)
            for b in range(B - 2):
                take_values(b)
                take_rest(b)
                if b + 3 < B:
                    norm_x(b + 3)
            for i in range(2):
                max_tile(0, i, 0)
                take_values(B - 2, banks=(i,))
            take_rest(B - 2)
            for i in range(2, TPB - 1):
                max_tile(0, i, 0)
            take_values(B - 1, banks=(0,))
            max_tile(0, TPB - 1, 0)
            take_values(B - 1, banks=(1,))
            max_end(0, 0)
            take_rest(B - 1)

            dve.wait_ge(table_T, TABLES)
            nc.vector.tensor_copy(centT[:], OB[:, 0:E]).then_inc(table_out, 1)
            nc.vector.tensor_copy(gbT[:], OB[:, 64:64 + 2 * E]).then_inc(table_out, 1)

            def invert_sums(pair, r):
                dve.wait_ge(oT_copied, pair + 1)
                ge(dve, o_normed, pair)
                nc.vector.reciprocal(rec[:], OT_s[:, r].rearrange("p (t c) -> p t c", c=VC)[:, :, 2 * DK:2 * DK + 2]
                                     ).then_inc(o_rec, 1)

            def slot(q, j):
                u = q * SLOTS + j
                for i in range(TPB):
                    max_tile(u + 2, i, j)
                    if i == 0:
                        max_end(u + 1, (j + 1) % 2)
                    if i == 6 and j % 2 == 0 and not (isinstance(u, int) and u == 0):
                        invert_sums(q * 2 + j // 2 - 1, (j // 2 + 1) % 2)

            for i in range(TPB):
                max_tile(1, i, 1)
            for j in range(SLOTS):
                slot(0, j)
            with dve.Fori(1, QUADS - 1) as q:
                for j in range(SLOTS):
                    slot(q, j)
            for j in range(SLOTS - 2):
                slot(QUADS - 1, j)
            max_end(NU - 1, 1)

            def take_aT(b, c):
                dve.wait_ge(a_ps, 2 * b + c + 1)
                nc.vector.tensor_copy(xnT[:, c * HALF:(c + 1) * HALF], SC[c][:]).then_inc(a_sb, 1)

            def add_attention(b):
                for c in range(2):
                    take_aT(b, c)
                for c in range(2):
                    dve.wait_ge(y_ps, 2 * b + c + 1)
                    xh = X[:, b * TPB + 4 * c:b * TPB + 4 * c + 4].rearrange("p t d -> p (t d)")
                    nc.vector.tensor_tensor(xh, xh, SC[c][:], ALU.add).then_inc(x1_ok, 1)
                dve.wait_ge(x1_ok, 2 * b + 2)

            step = chain(dve, dve_step, B * LN_STEPS)

            def take_stats(src, kind, b):
                for t in range(TPB):
                    last = nc.vector.bn_stats(stats[:, t], src[:, b * TPB + t])
                step(last)
                for t in range(TPB):
                    last = nc.vector.bn_aggr(mv2[:, kind, b * TPB + t], stats[:, t])
                step(last)

            def add_eps(k):
                kind, first, last = NORMS[k]
                nc.vector.tensor_scalar(vpe2[:, kind, first:last], mv2[:, kind, first:last, 1], EPS, None,
                                        ALU.add).then_inc(var_ok, 1)

            def take_coefs(k):
                kind, first, last = NORMS[k]
                vp, rt, sc, nw, sh = (m[:, kind, first:last] for m in (vpe2, root2, scale2, newt2, shift2))
                dve.wait_ge(root_ok, B + k + 1)
                step(nc.vector.reciprocal(sc, rt))
                step(nc.vector.tensor_tensor(nw, sc, sc, ALU.mult))
                step(nc.vector.tensor_tensor(nw, nw, vp, ALU.mult))
                step(nc.vector.tensor_scalar(nw, nw, -0.5, 1.5, ALU.mult, ALU.add))
                step(nc.vector.tensor_tensor(sc, sc, nw, ALU.mult))
                nc.vector.scalar_tensor_tensor(sh, mv2[:, kind, first:last, 0], -1.0, sc, ALU.mult, ALU.mult
                                               ).then_inc(coef_ok, 1)

            dve.wait_ge(bo_ok, B)
            for b in range(B - 1):
                add_attention(b)
                take_stats(X, U, b)
                if b == 1:
                    invert_sums(NPAIR - 2, 0)
            add_eps(0)
            take_coefs(0)
            invert_sums(NPAIR - 1, 1)
            add_attention(B - 1)

            def take_uT(b):
                dve.wait_ge(u_ps, 2 * b + 1)
                ge(dve, aff_ps, b - 1)
                nc.vector.tensor_copy(probs[:, b % 2, 0:HALF], OB[:]).then_inc(u_sb, 1)

            def take_aff(b):
                dve.wait_ge(aff_ps, b + 1)
                nc.vector.tensor_copy(aff[:, b * TPB:(b + 1) * TPB],
                                      ST[b % 2][:, 0:TPB * E].rearrange("p (t e) -> p t e", e=E)).then_inc(aff_ok, 1)
                dve.wait_ge(aff_ok, b + 1)
                nc.vector.tensor_reduce(sent[:, b * TPB:(b + 1) * TPB, 2 * D], aff[:, b * TPB:(b + 1) * TPB],
                                        axis=AX.X, op=ALU.max).then_inc(top_ok, 1)

            dve.wait_ge(v_ready, NU)
            take_uT(0)
            take_stats(X, U, B - 1)
            add_eps(1)
            take_coefs(1)
            for b in range(B):
                if b + 1 < B:
                    take_uT(b + 1)
                if b + 1 < B:
                    wait_u(dve, b)
                    take_stats(U2, XN, b)
                    add_eps(2 + b)
                take_aff(b)
                if b + 1 < B:
                    take_coefs(2 + b)

            dve.wait_ge(top_ok, B)
            step(nc.vector.tensor_tensor(eq[:], aff[:], sent[:, :, 2 * D:ROW].to_broadcast([P, T, E]), ALU.is_ge))
            step(nc.vector.tensor_tensor(eq[:], eq[:], first_w[:].unsqueeze(1).to_broadcast([P, T, E]), ALU.mult))
            step(nc.vector.tensor_reduce(pick[:], eq[:], axis=AX.X, op=ALU.max))
            step(nc.vector.tensor_tensor(hot[:], eq[:], pick[:].unsqueeze(2).to_broadcast([P, T, E]), ALU.is_equal))
            nc.vector.tensor_copy(hotb[:], hot[:]).then_inc(hot_ok, 1)
            take_stats(U2, XN, B - 1)
            add_eps(len(NORMS) - 1)
            take_coefs(len(NORMS) - 1)
            dve.wait_ge(rank_ps, 1)
            step(nc.vector.tensor_copy(tot[:], SC[1][:, 0:T * E].rearrange("p (t e) -> p e t", e=E)))
            flat = "p e t -> p (e t)"
            step(nc.vector.tensor_tensor_scan(cum[:].rearrange(flat), tot[:].rearrange(flat), zrow[:], 0.0, ALU.add, ALU.add))
            step(nc.vector.tensor_tensor(cum[:], cum[:], tot[:], ALU.subtract))
            step(nc.vector.tensor_reduce(cnt[:], tot[:], axis=AX.X, op=ALU.add))
            step(nc.vector.tensor_scalar(cnt[:], cnt[:], float(P - 1), None, ALU.add))
            step(nc.vector.tensor_copy(cnti[:], cnt[:]))
            step(nc.vector.tensor_scalar(cnti[:], cnti[:], 7, 7, ALU.logical_shift_right, ALU.logical_shift_left))
            step(nc.vector.tensor_copy(padded[:], cnti[:]))
            step(nc.vector.tensor_tensor_scan(ends[:], padded[:], zrow[:, 0:E], 0.0, ALU.add, ALU.add))
            step(nc.vector.tensor_tensor(start[:], ends[:], padded[:], ALU.subtract))
            step(nc.vector.tensor_tensor(cstart[:], start[:], cum[:, :, 0], ALU.subtract))
            step(nc.vector.tensor_tensor(cum[:], cum[:], cstart[:].unsqueeze(2).to_broadcast([P, E, T]), ALU.add))
            step(nc.vector.tensor_tensor(place[:], SC[0][:, 0:T * E].rearrange("p (t e) -> p t e", e=E),
                                         cum[:].rearrange("p e t -> p t e"), ALU.add))
            step(nc.vector.tensor_tensor(place[:], place[:], hot[:], ALU.mult))
            step(nc.vector.tensor_reduce(slot_f[:], place[:], axis=AX.X, op=ALU.add))
            step(nc.vector.tensor_copy(slot_i[:], slot_f[:]))
            step(nc.vector.tensor_scalar(slot_i[:], slot_i[:], 7, None, ALU.logical_shift_right))
            step(nc.vector.tensor_copy(slot_page[:], slot_i[:]))
            nc.vector.tensor_tensor(page_one, page[:].unsqueeze(1).to_broadcast([P, T, SORTED]),
                                    slot_page[:].unsqueeze(2).to_broadcast([P, T, SORTED]), ALU.is_equal).then_inc(dve_step, 1)
            step.count[0] += 1
            step(nc.vector.scalar_tensor_tensor(slot_at[:], slot_page[:], -float(P), slot_f[:], ALU.mult, ALU.add))
            nc.vector.tensor_tensor(page_id[:, :, 0], page_one, tile1[:].unsqueeze(2).to_broadcast([P, T, SORTED]),
                                    ALU.mult).then_inc(ones_ok, 1)
            nc.vector.tensor_scalar(page_id[:, :, 1], page_one, pcol[:], None, ALU.mult).then_inc(ones_ok, 1)
            for b in range(B):
                nc.vector.tensor_tensor(at_one[:, b * TPB:(b + 1) * TPB], prow[:].unsqueeze(1).to_broadcast([P, TPB, P]),
                                        slot_at[:, b * TPB:(b + 1) * TPB].unsqueeze(2).to_broadcast([P, TPB, P]),
                                        ALU.is_equal).then_inc(ones_ok, 1)
            dve.wait_ge(token_ps, 1)
            tile_sum, part_sum = OB[:, 0:SORTED], OB[:, SORTED:2 * SORTED]
            nc.vector.tensor_scalar(vacant[:], tile_sum, 0.0, float(2 * T * P), ALU.is_equal, ALU.mult).then_inc(dve_step, 1)
            step.count[0] += 1
            step(nc.vector.tensor_scalar(token_f[:], tile_sum, float(P), -float(P), ALU.mult, ALU.add))
            step(nc.vector.tensor_tensor(token_f[:], token_f[:], part_sum, ALU.add))
            step(nc.vector.tensor_tensor(token_f[:], token_f[:], vacant[:], ALU.add))
            nc.vector.tensor_copy(token[:], token_f[:]).then_inc(token_ok, 1)

            def take_from(n, q, j):
                bare(dve, (token_ok, 1), (xs_in[j], q * 16))
                nc.vector.tensor_copy(token_from[:, j:j + 1], token[:, bass.ds(n, 1)]).then_inc(from_ok, 1)

            dve.wait_ge(token_ok, 1)
            for n in range(5):
                take_from(n, 0, n)
            step(nc.vector.tensor_tensor(tile_cmp[:], tile_at[:].unsqueeze(2).to_broadcast([P, SORTED, E]),
                                         start[:].unsqueeze(1).to_broadcast([P, SORTED, E]), ALU.is_ge))
            step(nc.vector.tensor_reduce(tile_ef[:], tile_cmp[:], axis=AX.X, op=ALU.add))
            step(nc.vector.tensor_scalar(tile_ef[:], tile_ef[:], -1.0, None, ALU.add))
            nc.vector.tensor_copy(tile_e[:], tile_ef[:]).then_inc(slots_ok, 1)
            dve.wait_ge(ffn_in, 16 * FFN_LOADS)
            dve.wait_ge(b1_in, 16)
            dve.wait_ge(slots_ok, 1)

            def add_b1(n, i):
                e = dve.value_load(tile_e[0:1, bass.ds(n, 1)], min_val=0, max_val=E - 1)
                dve.wait_ge(h_ps, n + 1)
                nc.vector.tensor_tensor(hs[:, i], ST[i][:, 0:HALF], b1_s[:, bass.ds(e * F, F)],
                                        ALU.add).then_inc(h_sb, 1)

            def finish(n, i, q, j):
                e = dve.value_load(tile_e[0:1, bass.ds(n, 1)], min_val=0, max_val=E - 1)
                dve.wait_ge(f_ps, n + 1)
                ge(dve, f_sb, n)
                nc.vector.tensor_tensor(yb[:], (OB, MB)[i][:, 0:D], b2_s[:, bass.ds(e * D, D)],
                                        ALU.add).then_inc(yb_ok, 1)
                bare(dve, (token_ok, 1), (ys_out[j], q * 16))
                nc.vector.tensor_copy(token_to[:, j:j + 1], token[:, bass.ds(n, 1)]).then_inc(to_ok, 1)
                dve.wait_ge(yb_ok, n + 1)
                nc.vector.scalar_tensor_tensor(ys[:, j], yb[:], gate[:, j:j + 1], xs[:, j, D:2 * D],
                                               ALU.mult, ALU.add).then_inc(f_sb, 1)

            def step(n, q, j):
                if not isinstance(n, int) or n + 5 < SORTED:
                    take_from(n + 5, q + (j + 5) // RING, (j + 5) % RING)
                if not isinstance(n, int) or n < SORTED:
                    add_b1(n, j % 2)
                if not isinstance(n, int) or n >= 2:
                    finish(n - 2, j % 2, q + (j - 2) // RING, (j - 2) % RING)

            staged(dve, step)

        @block.tensor
        def _(pe):
            mm = nc.tensor.matmul
            pe.wait_ge(consts, CONSTS)
            pe.wait_ge(w_in, 16 * W_LOADS)
            def scores(n, i, j, halves=(0, 1)):
                for c in halves:
                    ge(pe, s_read, n * (2 * TPB) + 2 * i + c - 1)
                    mm(SC[c][:], QA[0:SHIFT, j, i * P:(i + 1) * P], KA[0:SHIFT, j, c * HALF:(c + 1) * HALF],
                       start=True, stop=True).then_inc(s_written, 1)

            def transpose_x(b):
                pe.wait_ge(normed, b + 1)
                for c in range(2):
                    ge(pe, xnT_sb, 2 * b)
                    for t in range(4):
                        last = nc.tensor.transpose(SC[c][:, t * P:(t + 1) * P], x_normed[:, b % 2 * TPB + 4 * c + t], ident[:])
                    last.then_inc(xnT_ps, 1)
                pe.wait_ge(xnT_sb, 2 * b + 2)

            def project_qk(b, i, halves=(0, 1)):
                ge(pe, full_ok, 2 * b)
                for c in halves:
                    last = mm(ST[i][:, c * HALF:(c + 1) * HALF], (wq_s, wk_s)[i][:], xnT[:, c * HALF:(c + 1) * HALF],
                              start=True, stop=True)
                if c == 1:
                    last.then_inc(qk_ps, 1)

            def project_v(b, c):
                ge(pe, v_ok, 2 * b)
                for t in range(4):
                    last = mm((OB, MB)[c][:, t * P:(t + 1) * P], xnT[:, (4 * c + t) * P:(4 * c + t + 1) * P], wv_s[:],
                              start=True, stop=True)
                last.then_inc(v_ps, 1)

            for b in range(B - 2):
                transpose_x(b)
                project_qk(b, 0)
                project_qk(b, 1)
                project_v(b, 0)
                project_v(b, 1)
            transpose_x(B - 2)
            project_qk(B - 2, 0)
            project_qk(B - 2, 1)
            pe.wait_ge(qk_loaded[0], 32)
            for i in range(2):
                scores(0, i, 0)
                project_v(B - 2, i)
            pe.wait_ge(s_read, 4)
            transpose_x(B - 1)
            for i in range(2, 6):
                scores(0, i, 0)
                project_qk(B - 1, (i - 2) // 2, halves=(i % 2,))
            for i in range(6, TPB):
                scores(0, i, 0)
                project_v(B - 1, i - 6)

            pe.wait_ge(v_ok, 2 * B)
            pe.wait_ge(table_in, 16 * 3)
            for at, src in ((0, cent_s), (64, gb_s)):
                n = src.shape[0]
                nc.tensor.transpose(OB[:, at:at + n], src[:], ident[0:n, 0:n]).then_inc(table_T, 1)
            pe.wait_ge(table_out, TABLES)

            def transpose_shift(n):
                pe.wait_ge(mparts_ready, n + 1)
                ge(pe, mT_copied, n)
                nc.tensor.transpose(MT, mparts[:].rearrange("p i t -> p (i t)"), identb[:]).then_inc(mT_written, 1)

            def scores_T(u, i, j):
                ge(pe, p_ready, u * TPB + i - 1)
                for c in range(2):
                    last = mm(ST[i % 2][:, c * HALF:(c + 1) * HALF], KA[:, j, i * P:(i + 1) * P],
                              QA[:, j, c * HALF:(c + 1) * HALF], start=True, stop=True)
                last.then_inc(st_written, 1)

            def weigh(u, i, j):
                pe.wait_ge(p_ready, u * TPB + i + 1)
                if i == 0:
                    pe.wait_ge(v_ready, u + 1)
                for g in range(4):
                    last = mm(OB[g * VC:(g + 1) * VC, 0:QUART], Vst[:, j, i, :],
                              probs[:, i % 2, g * QUART:(g + 1) * QUART],
                              start=(i == 0 and j % 2 == 0), stop=(i == TPB - 1 and j % 2 == 1))
                last.then_inc(pv_done, 1)

            def transpose_o(pair):
                pe.wait_ge(o_copied, pair + 1)
                ge(pe, oT_copied, pair)
                for c in range(2):
                    last = nc.tensor.transpose(MB[:, c * P:(c + 1) * P], O_s[:, c * P:(c + 1) * P], ident[:])
                last.then_inc(o_transposed, 1)

            def transpose_a(b, c):
                ge(pe, x1_ok, 2 * (b - 1) + c + 1)
                for t in range(4):
                    qt = 4 * c + t
                    last = nc.tensor.transpose(SC[c][:, t * P:(t + 1) * P], A[:, b * TPB + qt % 2 * 4 + qt // 2], ident[:])
                last.then_inc(a_ps, 1)

            def project_a(b, c):
                pe.wait_ge(a_sb, 2 * b + c + 1)
                for t in range(4 * c, 4 * c + 4):
                    last = mm(SC[c][:, t % 4 * P:(t % 4 + 1) * P], xnT[:, t * P:(t + 1) * P], wo_s[:], start=True, stop=True)
                last.then_inc(y_ps, 1)

            def add_batch(b, steps=range(4)):
                for n in steps:
                    if n == 0:
                        pe.wait_ge(o_normed, (b + 1) * (H // 2))
                        pe.wait_ge(s_read, NU * 2 * TPB)
                    (transpose_a, project_a)[n // 2](b, n % 2)

            def slot(q, j, last=False):
                u = q * SLOTS + j
                first = isinstance(u, int) and u == 0
                pe.wait_ge(shift_loaded[j], (q + 1) * (16 * PARTS))
                for i in range(TPB):
                    scores_T(u, i, j)
                    ahead = not (last and j >= 2)
                    if ahead and i == 0:
                        pe.wait_ge(qk_loaded[(j + 2) % SLOTS], (q + (j + 2) // SLOTS + 1) * 32)
                    if ahead:
                        scores(u + 2, i, (j + 2) % SLOTS, halves=(0,))
                    if i == 0 and not first:
                        weigh(u - 1, TPB - 1, (j - 1) % SLOTS)
                    if i == 1 and j % 2 == 0:
                        ge(pe, o_copied, q * 2 + j // 2)
                    if i > 0:
                        weigh(u, i - 1, j)
                    if ahead:
                        scores(u + 2, i, (j + 2) % SLOTS, halves=(1,))
                    if not ahead:
                        n = (j - 2) * TPB + i - 1
                        if 0 <= n < 4 * (B - 1):
                            add_batch(n // 4, [n % 4])
                    if i == SHIFT_AT and not (last and j == SLOTS - 1):
                        transpose_shift(u + 1)
                    if i == SHIFT_AT + 2 and j % 2 == 0 and not first:
                        pe.wait_ge(mT_copied, u + 2)
                        transpose_o(q * 2 + j // 2 - 1)

            pe.wait_ge(qk_loaded[1], 32)
            for i in range(TPB):
                scores(1, i, 1)
                if i == 0:
                    transpose_shift(0)
            for j in range(SLOTS):
                slot(0, j)
            with pe.Fori(1, QUADS - 1) as q:
                for j in range(SLOTS):
                    slot(q, j)
            for j in range(SLOTS):
                slot(QUADS - 1, j, last=True)
            weigh(NU - 1, TPB - 1, SLOTS - 1)
            transpose_o(NPAIR - 1)

            add_batch(B - 1)

            def transpose_u(b):
                wait_u(pe, b)
                ge(pe, u_sb, 2 * b)
                for c, bank in enumerate((OB, MB)):
                    for t in range(4):
                        last = nc.tensor.transpose(bank[:, t * P:(t + 1) * P], U2[:, b * TPB + 4 * c + t], ident[:])
                    last.then_inc(u_ps, 1)

            def affinities(b):
                pe.wait_ge(u_sb, 2 * b + 2)
                ge(pe, aff_ok, b - 1)
                for t in range(TPB):
                    last = mm(ST[b % 2][:, t * E:(t + 1) * E], probs[:, b % 2, t * P:(t + 1) * P], centT[:],
                              start=True, stop=True)
                last.then_inc(aff_ps, 1)

            transpose_u(0)
            for b in range(B):
                if b + 1 < B:
                    transpose_u(b + 1)
                affinities(b)

            pe.wait_ge(hot_ok, 1)
            mm(SC[0][:, 0:T * E], before[:], hotb[:].rearrange("p t e -> p (t e)"), start=True, stop=True)
            mm(SC[1][:, 0:T * E], onesb[:], hotb[:].rearrange("p t e -> p (t e)"), start=True, stop=True).then_inc(rank_ps, 1)
            for t in range(T):
                if t % TPB == 0:
                    pe.wait_ge(ones_ok, 3 + t // TPB)
                last = mm(OB[:, 0:2 * SORTED], at_one[:, t], page_id[:, t].rearrange("p i n -> p (i n)"),
                          start=(t == 0), stop=(t == T - 1))
            last.then_inc(token_ps, 1)

            pe.wait_ge(slots_ok, 1)
            pe.wait_ge(token_ok, 1)
            pe.wait_ge(ffn_in, 16 * FFN_LOADS)

            def take_x(n, i, q, j):
                pe.wait_ge(xs_in[j], q * 16 + 16)
                nc.tensor.transpose(SC[i][:, 0:P], xs[:, j, 0:D], ident[:]).then_inc(xs_ps, 1)

            def hidden(n, i, e):
                pe.wait_ge(xs_sb, n + 1)
                mm(ST[i][:, 0:HALF], xsT[:, i], w1_s[:, bass.ds(e * F, F)], start=True, stop=True).then_inc(h_ps, 1)

            def transpose_h(n, i):
                pe.wait_ge(h_sb, n + 1)
                for c in range(FC):
                    last = nc.tensor.transpose(ST[i][:, HALF + c * P:HALF + (c + 1) * P], hs[:, i, c * P:(c + 1) * P], ident[:])
                last.then_inc(ht_ps, 1)

            def project(n, i, e):
                pe.wait_ge(ht_sb, n + 1)
                ge(pe, yb_ok, n - 1)
                for c in range(FC):
                    last = mm((OB, MB)[i][:, 0:D], hT[:, i, c * P:(c + 1) * P], w2_s[:, bass.ds(e * F + c * D, D)],
                              start=(c == 0), stop=(c == FC - 1))
                last.then_inc(f_ps, 1)

            def expert(n):
                return pe.value_load(tile_e[0:1, bass.ds(n, 1)], min_val=0, max_val=E - 1)

            ahead = {}

            def step(n, q, j):
                i, known = j % 2, isinstance(n, int)
                if not known or n < SORTED:
                    e_hidden = ahead.pop((known, n if known else j), None)
                    if e_hidden is None:
                        e_hidden = expert(n)
                if not known or n + 1 < SORTED:
                    take_x(n + 1, 1 - i, q + (j + 1) // RING, (j + 1) % RING)
                if not known or n < SORTED:
                    hidden(n, i, e_hidden)
                if not known or n >= 2:
                    e_project = expert(n - 2)
                if j + 1 < RING and (not known or n + 1 < SORTED):
                    ahead[known, n + 1 if known else j + 1] = expert(n + 1)
                if not known or 0 <= n - 1 < SORTED:
                    transpose_h(n - 1, 1 - i)
                if not known or n >= 2:
                    project(n - 2, i, e_project)

            take_x(0, 0, 0, 0)
            staged(pe, step)


_INS = ['L0_attn_x', 'L0_attn_Wq', 'L0_attn_bq', 'L0_attn_Wk', 'L0_attn_bk', 'L0_attn_Wv', 'L0_attn_bv', 'L0_attn_Wo',
        'L0_attn_bo', 'L0_ffn_centroids', 'L0_ffn_ln_g', 'L0_ffn_ln_b', 'L0_ffn_w1', 'L0_ffn_b1', 'L0_ffn_w2', 'L0_ffn_b2']


def kernel(**inputs):
    import numpy as _np
    import concourse.bacc as _bacc
    from concourse import mybir as _mybir
    from concourse.bass_utils import run_bass_kernel_spmd as _run

    nc = _bacc.Bacc("TRN2", target_bir_lowering=False, num_devices=1)
    arrays, args = {}, []
    for name in _INS:
        a = _np.ascontiguousarray(inputs[name])
        arrays[f"in_{name}"] = a
        args.append(nc.dram_tensor(f"in_{name}", a.shape, _mybir.dt.from_np(a.dtype), kind="ExternalInput").ap())
    out = nc.dram_tensor("out_y", inputs["L0_attn_x"].shape, _mybir.dt.float32, kind="ExternalOutput").ap()
    build(nc, *args, out)
    r = _run(nc, [arrays], core_ids=[0])
    return r.results[0]["out_y"]
```
